# Optimizing a Trainium2 kernel written in Bass

```python
import numpy as np
import jax
import jax.numpy as jnp

def _softmax(x, axis=-1):
    return jax.nn.softmax(x, axis=axis)

def _gelu(x):
    return jax.nn.gelu(x, approximate=True)

def _silu(x):
    return jax.nn.silu(x)

def _sigmoid(x):
    return jax.nn.sigmoid(x)

def _layernorm(x, axis=-1, eps=1e-05):
    m = jnp.mean(x, axis=axis, keepdims=True)
    v = jnp.var(x, axis=axis, keepdims=True)
    return (x - m) / jnp.sqrt(v + eps)

def _scatter_add(tgt, idx, src, axis=0):
    return tgt.at[idx].add(src)

def _segment_sum(src, seg, n):
    return jax.ops.segment_sum(src, seg, n)
kernel_name = 'mk_xattn_seq_d1_seqx_r2_fa052a'

def setup_inputs(seed: int=0):
    np.random.seed(seed)
    _w = jnp.asarray

    def _rec_inputs():
        import jax
        import jax.numpy as jnp
        _rk = jax.random.key(seed)
        x = -0.0001233 + 1 * jax.random.normal(jax.random.fold_in(_rk, 1), (16, 512, 640), jnp.float32)
        _lenS = 512 - jax.random.randint(jax.random.fold_in(_rk, 7), (16,), 0, max(1, 512 // 4) + 1, jnp.int32)
        _lenS2 = 512 - jax.random.randint(jax.random.fold_in(_rk, 8), (16,), 0, max(1, 512 // 4) + 1, jnp.int32)
        _ctx_2048P = jax.random.normal(jax.random.fold_in(_rk, 11), (16, 16, 1024), jnp.float32)
        _ctx_2048c = jax.random.dirichlet(jax.random.fold_in(_rk, 511), 0.3 * jnp.ones((16,), jnp.float32), (16, 512))
        _ctx_2048t = jnp.einsum('bsk,bkd->bsd', _ctx_2048c, _ctx_2048P)
        _ctx_2048t = _ctx_2048t * jax.lax.rsqrt(jnp.mean(jnp.square(_ctx_2048t)) + 1e-12) * 0.953939
        ctx_2048 = 0.00266749 + 0.998873 * (_ctx_2048t + 0.3 * jax.random.normal(jax.random.fold_in(_rk, 611), (16, 512, 1024), jnp.float32))
        return (x, ctx_2048)
    x, ctx_2048 = _rec_inputs()

    def _L0_xattn_setup():
        import jax, jax.numpy as jnp
        import numpy as np
        B, S, C = (2, 2048, 640)
        CA = 1024
        HEADS = 20
        HD = C // HEADS
        N_TXT, N_OBJ, N_OTH, N_IP = (77, 4, 4, 16)
        SCALE_OBJ = SCALE_OTH = SCALE_IP = 1.0
        RESCALE = 1.0

        def _heads(x):
            b, l, _ = x.shape
            return x.reshape(b, l, HEADS, HD).transpose(0, 2, 1, 3)

        def _merge(x):
            b, h, l, d = x.shape
            return x.transpose(0, 2, 1, 3).reshape(b, l, h * d)

        def _sdpa(q, k, v):
            scale = 1.0 / np.sqrt(HD).astype(np.float32)
            s = jnp.einsum('bhqd,bhkd->bhqk', q, k) * scale
            p = jax.nn.softmax(s, axis=-1)
            return jnp.einsum('bhqk,bhkd->bhqd', p, v)
        key = jax.random.key(seed)
        ks = jax.random.split(key, 16)
        g = lambda k, shp, fan: jax.random.normal(k, shp, jnp.float32) / np.sqrt(fan).astype(np.float32)
        return {'hidden_states': jax.random.normal(ks[0], (B, S, C), jnp.float32), 'encoder_hidden_states': jax.random.normal(ks[1], (B, N_TXT + N_OBJ + N_OTH + N_IP, CA), jnp.float32), 'to_q_w': g(ks[2], (C, C), C), 'to_k_w': g(ks[3], (CA, C), CA), 'to_v_w': g(ks[4], (CA, C), CA), 'to_k_object_w': g(ks[5], (CA, C), CA), 'to_v_object_w': g(ks[6], (CA, C), CA), 'to_k_others_w': g(ks[7], (CA, C), CA), 'to_v_others_w': g(ks[8], (CA, C), CA), 'to_k_ip_w': g(ks[9], (CA, C), CA), 'to_v_ip_w': g(ks[10], (CA, C), CA), 'to_out_w': g(ks[11], (C, C), C), 'to_out_b': jnp.zeros((C,), jnp.float32)}
    _L0_xattn_all = _L0_xattn_setup()
    _L0_xattn_in = {k: v for k, v in _L0_xattn_all.items() if k in ('to_q_w', 'to_k_w', 'to_v_w', 'to_k_object_w', 'to_v_object_w', 'to_k_others_w', 'to_v_others_w', 'to_k_ip_w', 'to_v_ip_w', 'to_out_w', 'to_out_b')}
    del _L0_xattn_all
    return {'x': x, 'ctx_2048': ctx_2048, 'L0_xattn_to_q_w': _L0_xattn_in['to_q_w'], 'L0_xattn_to_k_w': _L0_xattn_in['to_k_w'], 'L0_xattn_to_v_w': _L0_xattn_in['to_v_w'], 'L0_xattn_to_k_object_w': _L0_xattn_in['to_k_object_w'], 'L0_xattn_to_v_object_w': _L0_xattn_in['to_v_object_w'], 'L0_xattn_to_k_others_w': _L0_xattn_in['to_k_others_w'], 'L0_xattn_to_v_others_w': _L0_xattn_in['to_v_others_w'], 'L0_xattn_to_k_ip_w': _L0_xattn_in['to_k_ip_w'], 'L0_xattn_to_v_ip_w': _L0_xattn_in['to_v_ip_w'], 'L0_xattn_to_out_w': _L0_xattn_in['to_out_w'], 'L0_xattn_to_out_b': _L0_xattn_in['to_out_b']}

def reference(x, ctx_2048, L0_xattn_to_q_w, L0_xattn_to_k_w, L0_xattn_to_v_w, L0_xattn_to_k_object_w, L0_xattn_to_v_object_w, L0_xattn_to_k_others_w, L0_xattn_to_v_others_w, L0_xattn_to_k_ip_w, L0_xattn_to_v_ip_w, L0_xattn_to_out_w, L0_xattn_to_out_b):
    import jax
    import jax.numpy as jnp

    def _L0_xattn_ref(hidden_states, encoder_hidden_states, to_q_w, to_k_w, to_v_w, to_k_object_w, to_v_object_w, to_k_others_w, to_v_others_w, to_k_ip_w, to_v_ip_w, to_out_w, to_out_b):
        import jax, jax.numpy as jnp
        import numpy as np
        B, S, C = (2, 2048, 640)
        CA = 1024
        HEADS = 20
        HD = C // HEADS
        N_TXT, N_OBJ, N_OTH, N_IP = (77, 4, 4, 16)
        SCALE_OBJ = SCALE_OTH = SCALE_IP = 1.0
        RESCALE = 1.0

        def _heads(x):
            b, l, _ = x.shape
            return x.reshape(b, l, HEADS, HD).transpose(0, 2, 1, 3)

        def _merge(x):
            b, h, l, d = x.shape
            return x.transpose(0, 2, 1, 3).reshape(b, l, h * d)

        def _sdpa(q, k, v):
            scale = 1.0 / np.sqrt(HD).astype(np.float32)
            s = jnp.einsum('bhqd,bhkd->bhqk', q, k) * scale
            p = jax.nn.softmax(s, axis=-1)
            return jnp.einsum('bhqk,bhkd->bhqd', p, v)
        residual = hidden_states
        end = N_TXT
        ehs_txt = encoder_hidden_states[:, :end]
        ehs_obj = encoder_hidden_states[:, end:end + N_OBJ]
        ehs_oth = encoder_hidden_states[:, end + N_OBJ:end + N_OBJ + N_OTH]
        ehs_ip = encoder_hidden_states[:, end + N_OBJ + N_OTH:]
        q = _heads(hidden_states @ to_q_w)
        h_txt = _sdpa(q, _heads(ehs_txt @ to_k_w), _heads(ehs_txt @ to_v_w))
        h_obj = _sdpa(q, _heads(ehs_obj @ to_k_object_w), _heads(ehs_obj @ to_v_object_w))
        h_oth = _sdpa(q, _heads(ehs_oth @ to_k_others_w), _heads(ehs_oth @ to_v_others_w))
        h_ip = _sdpa(q, _heads(ehs_ip @ to_k_ip_w), _heads(ehs_ip @ to_v_ip_w))
        out = _merge(h_txt) + SCALE_OBJ * _merge(h_obj) + SCALE_OTH * _merge(h_oth) + SCALE_IP * _merge(h_ip)
        out = out @ to_out_w + to_out_b
        out = (out + residual) / RESCALE
        return out
    x = _L0_xattn_ref(x, ctx_2048, L0_xattn_to_q_w, L0_xattn_to_k_w, L0_xattn_to_v_w, L0_xattn_to_k_object_w, L0_xattn_to_v_object_w, L0_xattn_to_k_others_w, L0_xattn_to_v_others_w, L0_xattn_to_k_ip_w, L0_xattn_to_v_ip_w, L0_xattn_to_out_w, L0_xattn_to_out_b)
    return x

_drawn_inputs = setup_inputs


def setup_inputs(seed=0):
    import zlib

    import numpy as np

    out = dict(_drawn_inputs(seed))
    spreads = {'L0_xattn_to_out_b': (0.0, 0.1)}
    factors = {}
    for name, (base, spread) in spreads.items():
        noise = np.random.default_rng([zlib.crc32(name.encode()), seed]).standard_normal(out[name].shape)
        drawn = base * np.exp(spread * noise) if base else spread * noise
        out[name] = jnp.asarray(drawn.astype(out[name].dtype))
    for name, factor in factors.items():
        out[name] = (out[name] * factor).astype(out[name].dtype)
    return out
```

```python
from contextlib import ExitStack

import concourse.bass as bass
from concourse import mybir

ALU = mybir.AluOpType
ACT = mybir.ActivationFunctionType
AX_X = mybir.AxisListType.X
F32 = mybir.dt.float32
F32R = mybir.dt.float32r
BF16 = mybir.dt.bfloat16

BATCH = 16
TOK = 512
CH = 640
CTX = 1024
HD = 32
P = 128
QC = CH // P
CC = CTX // P
HPU = P // HD
N_TXT, N_OBJ, N_OTH = 77, 4, 4
SMALL = N_TXT + N_OBJ + N_OTH
N_IP = TOK - SMALL
REST = P - SMALL
GROUPS = 4
SCALE = float(HD) ** -0.5

HI, LO = 0, 1
PASSES = ((HI, HI), (HI, LO), (LO, HI))

IPN = TOK - SMALL + 1
TXT_B = 4
REST_B = 8
N_TXT_RUNS = BATCH // TXT_B
N_REST_RUNS = BATCH // REST_B
RUN_OBJ = N_TXT_RUNS
RUN_OTH = RUN_OBJ + 1
RUN_REST = RUN_OTH + 1
RUN_IP = RUN_REST + N_REST_RUNS
RUNS = RUN_IP + BATCH
RAW = 4
WS = 3


def v_tiles(n):
    return [(a, min(P, n - a)) for a in range(0, n, P)]


def due(count):
    return not isinstance(count, int) or count > 0


def project_context(nc, d):
    with ExitStack() as ctx:
        def sb(name, shape, dt):
            return ctx.enter_context(nc.sbuf_tensor(name, shape, dt))

        def sem(name):
            return ctx.enter_context(nc.semaphore(name))

        w = sb("w_split", [P, WS, 2, CC, CH], F32R)
        c = sb("ctx_split", [P, 2, 2, CC, IPN], F32R)
        raw = sb("raw", [P, RAW, CH], F32)
        k_out = sb("k_out", [P, 2, 2, TOK], F32R)
        v_out = sb("v_out", [P, 2, CH], F32)
        k_ps = ctx.enter_context(nc.psum_tensor("k_ps", [P, 2, 512], F32))
        v_ps = ctx.enter_context(nc.psum_tensor("v_ps", [P, 2, 2, 512], F32))

        raw_in = [sem(f"raw_in{r}") for r in range(RAW)]
        piece_hi = sem("piece_hi")
        piece_lo = sem("piece_lo")
        k_acc = sem("k_acc")
        k_hi = sem("k_hi")
        k_lo = sem("k_lo")
        v_acc = sem("v_acc")
        v_sb = sem("v_sb")
        k_stored = [sem(f"k_stored{r}") for r in range(2)]
        v_stored = [sem(f"v_stored{r}") for r in range(2)]

        W_ORDER = [("k_txt", 0, -1), ("v_txt", 1, -1), ("k_obj", 2, 0), ("v_obj", 0, RUN_OBJ - 1),
                   ("k_oth", 1, RUN_OBJ - 1), ("v_oth", 2, RUN_OBJ), ("k_ip", 0, RUN_OBJ), ("v_ip", 1, RUN_OTH)]
        SLOT = {name: slot for name, slot, _ in W_ORDER}

        def group_of(run):
            return ("txt" if run < RUN_OBJ else "obj" if run < RUN_OTH else "oth" if run < RUN_REST else
                    "rest" if run < RUN_IP else "ip")

        def width(run):
            return {"txt": TXT_B * N_TXT, "obj": BATCH * N_OBJ, "oth": BATCH * N_OTH, "rest": REST_B * REST,
                    "ip": IPN}[group_of(run)]

        def k_blocks(run):
            return 0 if group_of(run) == "rest" else QC

        def tiles(run):
            if group_of(run) == "ip":
                return [(P * (t + 1) - SMALL + 1, P) for t in range(TOK // P - 1)]
            return v_tiles(width(run))

        k_base, v_base, lots = [0], [0], []
        for run in range(RUNS):
            k_base.append(k_base[-1] + k_blocks(run))
            v_base.append(v_base[-1] + len(tiles(run)))
        lots += [("w", "k_txt"), ("c", 0), ("w", "v_txt")]
        for run in range(RUNS - 1):
            lots += [("c", run + 1)] + [("w", name) for name, _, after in W_ORDER if after == run]
        LOT = {lot: n for n, lot in enumerate(lots)}

        def pieces_upto(kind, which):
            return CC * (LOT[(kind, which)] + 1)

        def ready(run):
            need = [pieces_upto("c", run)]
            g = "ip" if group_of(run) == "rest" else group_of(run)
            need += [pieces_upto("w", f"v_{g}")] + [pieces_upto("w", f"k_{g}")] * (k_blocks(run) > 0)
            return max(need)

        PER_TURN = 2
        TURNS = (BATCH - PER_TURN) // PER_TURN
        D_PIECE, D_K, D_V = PER_TURN * CC, PER_TURN * QC, PER_TURN * len(tiles(RUN_IP))

        def ctx_src(run0, i, n):
            g, rows = group_of(run0), slice(n * P, (n + 1) * P)
            if g == "ip":
                return d["ctxT"][run0 - RUN_IP + PER_TURN * i, rows, TOK - IPN:TOK]
            if g == "txt":
                return d["ctxT_txt"][rows, run0 * width(0):(run0 + 1) * width(0)]
            if g == "rest":
                return d["ctxT_rest"][rows, (run0 - RUN_REST) * width(run0):(run0 - RUN_REST + 1) * width(run0)]
            return d[f"ctxT_{g}"][rows, :]

        def in_turns(eng, one_run):
            for run in range(RUN_IP):
                one_run(run, 0)
            with eng.Fori(0, TURNS) as i:
                for run in range(RUN_IP, RUN_IP + PER_TURN):
                    one_run(run, i)
            for run in range(RUNS - PER_TURN, RUNS):
                one_run(run, 0)

        block = ctx.enter_context(nc.Block())

        @block.sync
        def _(sp):
            def load(k0, i, src):
                if due(n_due := k0 - RAW + 1 + D_PIECE * i):
                    sp.wait_ge(piece_lo, n_due)
                sp.dma_start(raw[:, k0 % RAW, 0:src.shape[-1]], src).then_inc(raw_in[k0 % RAW], 16)

            def load_w(name):
                for n in range(CC):
                    load(CC * LOT[("w", name)] + n, 0, d[name][n * P:(n + 1) * P, :])

            load_w("k_txt")
            for n in range(CC):
                load(CC * LOT[("c", 0)] + n, 0, ctx_src(0, 0, n))
            load_w("v_txt")

            def store_k(run0, i, m):
                k0, g, n = k_base[run0] + m, group_of(run0), width(run0)
                sp.wait_ge(k_lo, k0 + 1 + D_K * i)
                for part in (HI, LO):
                    rows = slice(m * P, (m + 1) * P)
                    if g == "ip":
                        dst = d["kT"][run0 - RUN_IP + PER_TURN * i, part, rows, SMALL:TOK]
                        src = k_out[:, k0 % 2, part, 1:n]
                    else:
                        at, size = {"txt": (0, N_TXT), "obj": (N_TXT, N_OBJ), "oth": (N_TXT + N_OBJ, N_OTH)}[g]
                        b0 = TXT_B * run0 if g == "txt" else 0
                        dst = d["kT"][b0:b0 + n // size, part, rows, at:at + size].rearrange("b p t -> p b t")
                        src = k_out[:, k0 % 2, part, 0:n].rearrange("p (b t) -> p b t", t=size)
                    sp.dma_start(dst, src.bitcast(F32)).then_inc(k_stored[k0 % 2], 16)

            def store_v(run0, i, t):
                v0, g, (a, rows) = v_base[run0] + t, group_of(run0), tiles(run0)[t]
                if g == "ip":
                    dst = d["v_ip_rows"][run0 - RUN_IP + PER_TURN * i, t * P:(t + 1) * P, :]
                else:
                    a += {"txt": run0, "rest": run0 - RUN_REST}.get(g, 0) * width(run0)
                    dst = d[f"v_{g}_rows"][a:a + rows, :]
                sp.wait_ge(v_sb, v0 + 1 + D_V * i)
                sp.dma_start(dst, v_out[0:rows, v0 % 2, :]).then_inc(v_stored[v0 % 2], 16)

            def one_run(run0, i):
                blocks = k_blocks(run0)
                for n in range(CC):
                    if run0 < RUNS - 1:
                        load(CC * LOT[("c", run0 + 1)] + n, i, ctx_src(run0 + 1, i, n))
                    if n < blocks:
                        store_k(run0, i, n)
                    elif n - blocks < len(tiles(run0)):
                        store_v(run0, i, n - blocks)
                for name, _, after in W_ORDER:
                    if after == run0:
                        load_w(name)

            in_turns(sp, one_run)
            for r in range(2):
                sp.wait_ge(k_stored[r], 32 * ((k_base[RUNS] - r + 1) // 2))
                sp.wait_ge(v_stored[r], 16 * ((v_base[RUNS] - r + 1) // 2))

        @block.scalar
        def _(act):
            def split_hi(k0, i, dst, n):
                act.wait_ge(raw_in[k0 % RAW], 16 * (k0 // RAW + 1) + 16 * (D_PIECE // RAW) * i)
                nc.scalar.activation(dst, raw[:, k0 % RAW, 0:n], ACT.Copy).then_inc(piece_hi, 1)

            def split_ctx(run0, i, n):
                if n == 0:
                    if due(n_due := v_base[max(run0 - 1, 0)] + D_V * i):
                        act.wait_ge(v_acc, n_due)
                split_hi(CC * LOT[("c", run0)] + n, i, c[:, run0 % 2, HI, n, 0:width(run0)], width(run0))

            def split_w(name, after):
                if due(n_due := v_base[after + 1]):
                    act.wait_ge(v_acc, n_due)
                for n in range(CC):
                    split_hi(CC * LOT[("w", name)] + n, 0, w[:, SLOT[name], HI, n, :], CH)

            split_w("k_txt", -1)
            for n in range(CC):
                split_ctx(0, 0, n)
            split_w("v_txt", -1)

            def keep_k(run0, i, m):
                k0, n = k_base[run0] + m, width(run0)
                act.wait_ge(k_acc, k0 + 1 + D_K * i)
                if due(n_due := 32 * (k0 // 2) + 16 * D_K * i):
                    act.wait_ge(k_stored[k0 % 2], n_due)
                nc.scalar.activation(k_out[:, k0 % 2, HI, 0:n], k_ps[:, k0 % 2, 0:n], ACT.Copy).then_inc(k_hi, 1)

            def keep_v(run0, i, t):
                v0, rows = v_base[run0] + t, tiles(run0)[t][1]
                act.wait_ge(v_acc, v0 + 1 + D_V * i)
                if due(n_due := 16 * (v0 // 2) + 8 * D_V * i):
                    act.wait_ge(v_stored[v0 % 2], n_due)
                nc.scalar.activation(v_out[0:rows, v0 % 2, :].rearrange("p (a n) -> p a n", a=2),
                                     v_ps[0:rows, v0 % 2, :, 0:CH // 2], ACT.Copy).then_inc(v_sb, 1)

            def one_run(run0, i):
                blocks = k_blocks(run0)
                for n in range(CC):
                    if run0 < RUNS - 1:
                        split_ctx(run0 + 1, i, n)
                    if n < blocks:
                        keep_k(run0, i, n)
                    elif n - blocks < len(tiles(run0)):
                        keep_v(run0, i, n - blocks)
                for name, _, after in W_ORDER:
                    if after == run0:
                        split_w(name, after)

            in_turns(act, one_run)

        @block.vector
        def _(dve):
            def split_lo(k0, i, hi, lo, n):
                dve.wait_ge(piece_hi, k0 + 1 + D_PIECE * i)
                nc.vector.tensor_tensor(lo, raw[:, k0 % RAW, 0:n], hi.bitcast(F32), ALU.subtract).then_inc(piece_lo, 1)

            def split_ctx(run0, i, n):
                b, wd = run0 % 2, width(run0)
                split_lo(CC * LOT[("c", run0)] + n, i, c[:, b, HI, n, 0:wd], c[:, b, LO, n, 0:wd], wd)

            def split_w(name):
                s = SLOT[name]
                for n in range(CC):
                    split_lo(CC * LOT[("w", name)] + n, 0, w[:, s, HI, n, :], w[:, s, LO, n, :], CH)

            split_w("k_txt")
            for n in range(CC):
                split_ctx(0, 0, n)
            split_w("v_txt")

            def keep_k(run0, i, m):
                k0, n = k_base[run0] + m, width(run0)
                dve.wait_ge(k_hi, k0 + 1 + D_K * i)
                nc.vector.tensor_tensor(k_out[:, k0 % 2, LO, 0:n], k_ps[:, k0 % 2, 0:n],
                                        k_out[:, k0 % 2, HI, 0:n].bitcast(F32), ALU.subtract).then_inc(k_lo, 1)

            def one_run(run0, i):
                for n in range(CC):
                    if run0 < RUNS - 1:
                        split_ctx(run0 + 1, i, n)
                    if n < k_blocks(run0):
                        keep_k(run0, i, n)
                for name, _, after in W_ORDER:
                    if after == run0:
                        split_w(name)

            in_turns(dve, one_run)

        @block.tensor
        def _(pe):
            def one_run(run0, i):
                g, n, b = group_of(run0), width(run0), run0 % 2
                wg = "ip" if g == "rest" else g
                pe.wait_ge(piece_lo, ready(run0) + D_PIECE * i)
                for m in range(k_blocks(run0)):
                    k0, s = k_base[run0] + m, SLOT[f"k_{wg}"]
                    if due(n_due := k0 - 1 + D_K * i):
                        pe.wait_ge(k_lo, n_due)
                    for q in range(CC):
                        for z, (pw, px) in enumerate(PASSES):
                            last = nc.tensor.matmul(k_ps[:, k0 % 2, 0:n], w[:, s, pw, q, m * P:(m + 1) * P],
                                                    c[:, b, px, q, 0:n], start=(q == 0 and z == 0),
                                                    stop=(q == CC - 1 and z == len(PASSES) - 1))
                    last.then_inc(k_acc, 1)
                s = SLOT[f"v_{wg}"]
                for t, (a, rows) in enumerate(tiles(run0)):
                    v0 = v_base[run0] + t
                    if due(n_due := v0 - 1 + D_V * i):
                        pe.wait_ge(v_sb, n_due)
                    for half in range(2):
                        for q in range(CC):
                            for z, (px, pw) in enumerate(PASSES):
                                last = nc.tensor.matmul(
                                    v_ps[0:rows, v0 % 2, half, 0:CH // 2], c[:, b, px, q, a:a + rows],
                                    w[:, s, pw, q, half * (CH // 2):(half + 1) * (CH // 2)],
                                    start=(q == 0 and z == 0), stop=(q == CC - 1 and z == len(PASSES) - 1))
                    last.then_inc(v_acc, 1)

            in_turns(pe, one_run)


UNITS = BATCH * QC
RING = 3
LOOP = RING * QC
STEPS = 8
QT = TOK // P
KT = TOK // P
PAIRS = HPU * QT // 2
ITEMS = HPU * KT
PR = 8
XR = 3
ROWS_S = 3 * HD
ROWS_ST = ROWS_S + 2 * GROUPS
BLOCKS = ((HI, HI), (LO, HI), (HI, LO))
IP = GROUPS - 1
Y_STEPS = range(2, 2 + QC)
LAST_LAG = 5


def attend(nc, d):
    with ExitStack() as ctx:
        def sb(name, shape, dt):
            return ctx.enter_context(nc.sbuf_tensor(name, shape, dt))

        def psum(name, shape):
            return ctx.enter_context(nc.psum_tensor(name, shape, F32))

        def sem(name):
            return ctx.enter_context(nc.semaphore(name))

        wq = sb("wq", [P, 2, QC, CH], F32R)
        wo = sb("wo", [P, 2, QC, CH], F32R)
        xraw = sb("xraw", [P, XR, CH], F32)
        xs = sb("xs", [P, 2, QC, TOK], F32R)
        q_out = sb("q_out", [P, 2, TOK], F32R)
        qpack = sb("qpack", [P, RING, HPU, TOK], F32R)
        kpack = sb("kpack", [P, RING, HPU, TOK], F32R)
        group_rows = sb("group_rows", [P, TOK], F32)
        vt = sb("vt", [P, RING, KT, P], F32)
        small = sb("small", [P, HPU * QT, SMALL], F32)
        negmax = sb("negmax", [P, RING, QT, GROUPS, HPU], F32)
        sums = sb("sums", [P, RING, QT, GROUPS, HPU], F32)
        logs = sb("logs", [P, QT, GROUPS, HPU], F32)
        neglse = sb("neglse", [P, QT, GROUPS, HPU], F32)
        neglse2 = sb("neglse2", [P, QT, 2, GROUPS, HPU], F32R)
        lse_rows = sb("lse_rows", [2 * GROUPS * HPU, TOK], F32R)
        unused = sb("unused", [P, 2, 2, N_IP], BF16)
        probs = sb("probs", [P, PR, TOK], F32)
        heads = sb("heads", [P, RING, 2, TOK], F32R)
        acc = sb("acc", [P, QC, TOK], F32)
        ident = sb("ident", [P, P], F32)
        bias = sb("bias", [P, QC], F32)

        s_ps = psum("s_ps", [P, 2, 2, 512])
        st_ps = psum("st_ps", [P, 2, 512])
        o_ps = psum("o_ps", [P, 512])
        m_ps = psum("m_ps", [P, 512])

        const_in = sem("const_in")
        raw_in = [sem(f"raw2_in{r}") for r in range(XR)]
        x_hi, x_lo = sem("x_hi"), sem("x_lo")
        rows_set = sem("rows_set")
        q_acc, q_hi, q_lo = sem("q_acc"), sem("q_hi"), sem("q_lo")
        q_packed = [sem(f"q_packed{r}") for r in range(RING)]
        k_packed = [sem(f"k_packed{r}") for r in range(RING)]
        v_in = [sem(f"v_in{r}") for r in range(RING)]
        s_done = sem("s_done")
        s_max = sem("s_max")
        s_exp = sem("s_exp")
        row_max = sem("row_max")
        sm_sub = sem("sm_sub")
        sm_exp = sem("sm_exp")
        sm_sum = sem("sm_sum")
        ln_done = sem("ln_done")
        lse_step = sem("lse_step")
        lse_t = sem("lse_t")
        lse_sb = sem("lse_sb")
        lse_packed = [sem(f"lse_packed{r}") for r in range(RING)]
        st_done = sem("st_done")
        p_done = sem("p_done")
        pv_done = sem("pv_done")
        o_hi, o_lo = sem("o_hi"), sem("o_lo")
        y_done = sem("y_done")
        y_added = sem("y_added")
        res_in = [sem(f"res_in{c}") for c in range(QC)]
        y_out = [sem(f"y_out{c}") for c in range(QC)]

        def count(per, k, i, more=0):
            return per * k + more + per * LOOP * i

        def use(k, i):
            return k // RING + 1 + (LOOP // RING) * i

        def batch(k, i):
            return k // QC + (LOOP // QC) * i

        def there(k, i):
            return 0 <= k < UNITS if isinstance(i, int) else True

        PRELUDE = LAST_LAG
        TURNS = (UNITS - PRELUDE) // LOOP
        assert PRELUDE + TURNS * LOOP == UNITS

        def in_slots(eng, slot):
            for m in range(PRELUDE):
                slot(m, 0)
            with eng.Fori(0, TURNS) as i:
                for m in range(PRELUDE, PRELUDE + LOOP):
                    slot(m, i)
            for m in range(UNITS, UNITS + LAST_LAG):
                slot(m, 0)

        def pair_at(m, k):
            return (m - 1, k - 6) if k >= 6 else (m - 2, k + 2)

        def items_at(m, k):
            u, at = (m - 3, k - 3) if k >= 3 else (m - 4, k + 5)
            return u, (2 * at, 2 * at + 1)

        PIECES_W = 2 * QC

        def piece(k, i, c):
            return PIECES_W + k + c

        block = ctx.enter_context(nc.Block())

        @block.sync
        def _(sp):
            sp.dma_start(ident[:, :], d["ident"]).then_inc(const_in, 16)
            sp.dma_start(bias[:, :], d["bias"]).then_inc(const_in, 16)
            sp.dma_start(group_rows[ROWS_S:ROWS_ST, :], d["group_rows"]).then_inc(const_in, 16)

            def load(n, i, src):
                if due(n_due := n - XR + 1 + LOOP * i):
                    sp.wait_ge(x_lo, n_due)
                sp.dma_start(xraw[:, n % XR, 0:src.shape[-1]], src).then_inc(raw_in[n % XR], 16)

            for c in range(QC):
                sp.dma_start(acc[:, c, :], d["xT"][0, c * P:(c + 1) * P, :]).then_inc(res_in[c], 16)
            for z, name in enumerate(("wq", "wo")):
                for c in range(QC):
                    load(z * QC + c, 0, d[name][c * P:(c + 1) * P, :])

            def pack(u, i):
                r, b, cols = u % RING, batch(u, i), slice(u % QC * P, (u % QC + 1) * P)
                if due(n_due := count(ITEMS, u - RING + 1, i)):
                    sp.wait_ge(st_done, n_due)
                for n, (_, part) in enumerate(BLOCKS):
                    sp.dma_start(kpack[n * HD:(n + 1) * HD, r, :, :].bitcast(F32),
                                 d["kT"][b, part, cols, :].rearrange("(j c) t -> c j t", c=HD)).then_inc(k_packed[r], 16)
                sp.wait_ge(q_lo, count(1, u, i, 1))
                for n, (part, _) in enumerate(BLOCKS):
                    for j in range(HPU):
                        sp.dma_start(qpack[n * HD:(n + 1) * HD, r, j, :].bitcast(F32),
                                     q_out[j * HD:(j + 1) * HD, part, :].bitcast(F32)).then_inc(q_packed[r], 16)
                if due(n_due := count(KT, u - RING + 1, i)):
                    sp.wait_ge(pv_done, n_due)
                row = 0
                for g, n in (("txt", N_TXT), ("obj", N_OBJ), ("oth", N_OTH), ("rest", REST)):
                    sp.dma_start(vt[row:row + n, r, 0, :], d[f"v_{g}_rows"][bass.ds(b * n, n), cols]).then_inc(v_in[r], 16)
                    row += n
                sp.dma_start(vt[:, r, 1:KT, :], d["v_ip_rows"][b, :, cols].rearrange("(t p) n -> p t n", p=P))\
                    .then_inc(v_in[r], 16)

            def slot(m, i):
                if m % QC == 0 and there(m, i):
                    for c in range(QC):
                        load(piece(m, i, c), i, d["xT"][batch(m, i), c * P:(c + 1) * P, :])
                u = m - 3
                if there(u, i):
                    sp.wait_ge(lse_sb, count(1, u, i, 1))
                    sp.dma_start(qpack[ROWS_S:ROWS_ST, u % RING, :, :].bitcast(F32), lse_rows[:, :].bitcast(F32)).then_inc(lse_packed[u % RING], 16)
                if there(m - 1, i):
                    pack(m - 1, i)
                u = m - 5
                if there(u, i) and u % QC == QC - 1:
                    b = batch(u, i)
                    for c in range(QC):
                        sp.wait_ge(y_added, count(QC, u, i, c + 1))
                        sp.dma_start(d["yT"][b, c * P:(c + 1) * P, :], acc[:, c, :]).then_inc(y_out[c], 16)
                    if m < UNITS + LAST_LAG - 1:
                        for c in range(QC):
                            sp.wait_ge(y_out[c], 16 * (b + 1))
                            sp.dma_start(acc[:, c, :], d["xT"][b + 1, c * P:(c + 1) * P, :]).then_inc(res_in[c], 16)

            in_slots(sp, slot)
            for c in range(QC):
                sp.wait_ge(y_out[c], 16 * BATCH)

        @block.gpsimd
        def _(pool):
            pool.wait_ge(const_in, 48)
            for r in range(RING):
                for j in range(HPU):
                    nc.gpsimd.tensor_copy(kpack[ROWS_S:ROWS_ST, r, j, :], group_rows[ROWS_S:ROWS_ST, :]).then_inc(rows_set, 1)

        @block.tensor
        def _(pe):
            pe.wait_ge(const_in, 48)
            pe.wait_ge(rows_set, RING * HPU)

            def scores(u, p, i):
                j, t0, n = p // 2, 2 * (p % 2), PAIRS * u + p
                if p == 0:
                    pe.wait_ge(q_packed[u % RING], 16 * len(BLOCKS) * HPU * use(u, i))
                    pe.wait_ge(k_packed[u % RING], 16 * len(BLOCKS) * use(u, i))
                if due(n_due := count(PAIRS, u, i, p - 1)):
                    pe.wait_ge(s_exp, n_due)
                for z in range(2):
                    t = t0 + z
                    last = nc.tensor.matmul(s_ps[:, n % 2, z, :], qpack[0:ROWS_S, u % RING, j, t * P:(t + 1) * P],
                                            kpack[0:ROWS_S, u % RING, j, :], start=True, stop=True)
                last.then_inc(s_done, 1)

            def scores_t(u, items, i):
                r = u % RING
                if items[0] == 0:
                    pe.wait_ge(lse_packed[r], 16 * use(u, i))
                for x in items:
                    kt, j = x // HPU, x % HPU
                    if due(n_due := count(ITEMS, u, i, x - 1)):
                        pe.wait_ge(p_done, n_due)
                    nc.tensor.matmul(st_ps[:, x % 2, :], kpack[0:ROWS_ST, r, j, kt * P:(kt + 1) * P],
                                     qpack[0:ROWS_ST, r, j, :], start=True, stop=True).then_inc(st_done, 1)

            def values(u, kt, i):
                r = u % RING
                if kt == 0:
                    pe.wait_ge(v_in[r], 16 * 5 * use(u, i))
                    if due(n_due := count(1, u, i)):
                        pe.wait_ge(o_lo, n_due)
                pe.wait_ge(p_done, count(ITEMS, u, i, HPU * (kt + 1)))
                for j in range(HPU):
                    last = nc.tensor.matmul(o_ps[j * HD:(j + 1) * HD, :], vt[:, r, kt, j * HD:(j + 1) * HD],
                                            probs[:, (HPU * kt + j) % PR, :], start=(kt == 0), stop=(kt == KT - 1))
                last.then_inc(pv_done, 1)

            def queries(u, i, products):
                if products[0] == 0:
                    if due(n_due := count(QC, u - 4, i)):
                        pe.wait_ge(y_added, n_due)
                    pe.wait_ge(x_lo, piece(u // QC * QC, i, QC) + LOOP * i)
                cols = slice(u % QC * P, (u % QC + 1) * P)
                for n in products:
                    c, (pw, px) = n // len(PASSES), PASSES[n % len(PASSES)]
                    last = nc.tensor.matmul(m_ps[:, :], wq[:, pw, c, cols], xs[:, px, c, :], start=(n == 0),
                                            stop=(n == QC * len(PASSES) - 1))
                if products[-1] == QC * len(PASSES) - 1:
                    last.then_inc(q_acc, 1)

            def transpose_lse(u, i):
                pe.wait_ge(q_lo, count(1, u, i, 3) if there(u + 2, i) else UNITS)
                pe.wait_ge(lse_step, count(3, u, i, 3))
                for t in range(QT):
                    last = nc.tensor.transpose(m_ps[0:2 * GROUPS * HPU, t * P:(t + 1) * P],
                                               neglse2[:, t, :, :, :].bitcast(F32).rearrange("p a g j -> p (a g j)"),
                                               ident[:, :])
                last.then_inc(lse_t, 1)

            def output(u, i, c):
                if c == 0:
                    pe.wait_ge(o_lo, count(1, u, i, 1))
                    pe.wait_ge(lse_sb, count(1, u, i, 3) if there(u + 2, i) else UNITS)
                if c > 0 or not there(u + 2, i):
                    pe.wait_ge(y_added, count(QC, u, i, c))
                for n, (pw, po) in enumerate(PASSES):
                    last = nc.tensor.matmul(m_ps[:, :], wo[:, pw, u % QC, c * P:(c + 1) * P], heads[:, u % RING, po, :],
                                            start=(n == 0), stop=(n == len(PASSES) - 1))
                last.then_inc(y_done, 1)

            def slot(m, i):
                for k in range(STEPS):
                    u, p = pair_at(m, k)
                    if there(u, i):
                        scores(u, p, i)
                    u, items = items_at(m, k)
                    if there(u, i):
                        scores_t(u, items, i)
                    if k == 0 and there(m - 1, i):
                        queries(m - 1, i, range(10, QC * len(PASSES)))
                    if k == 1 and there(m - 3, i):
                        transpose_lse(m - 3, i)
                    if k in Y_STEPS and there(m - 5, i):
                        output(m - 5, i, k - Y_STEPS[0])
                    if k == 6 and there(m, i):
                        queries(m, i, range(0, 4))
                    if k == 7 and there(m, i):
                        queries(m, i, range(4, 10))
                    for at, lag, kt in ((5, 3, 0), (7, 3, 1), (1, 4, 2), (3, 4, 3)):
                        if k == at and there(m - lag, i):
                            values(m - lag, kt, i)

            in_slots(pe, slot)

        @block.scalar
        def _(act):
            def split_hi(n, i, dst, width):
                act.wait_ge(raw_in[n % XR], 16 * (n // XR + 1) + 16 * (LOOP // XR) * i)
                nc.scalar.activation(dst, xraw[:, n % XR, 0:width], ACT.Copy).then_inc(x_hi, 1)

            nc.scalar.preload_act_table_set("natural_log_exp_and_others")
            for z, w in enumerate((wq, wo)):
                for c in range(QC):
                    split_hi(z * QC + c, 0, w[:, HI, c, :], CH)

            def prob(u, items, i):
                for x in items:
                    act.wait_ge(st_done, count(ITEMS, u, i, x + 1))
                    if x % HPU == 0:
                        if due(n_due := count(KT, u, i, x // HPU - 1)):
                            act.wait_ge(pv_done, n_due)
                    nc.scalar.activation(probs[:, x % PR, :], st_ps[:, x % 2, :], ACT.Exp).then_inc(p_done, 1)

            def ip_sums(u, p, i):
                j, t0, n, r = p // 2, 2 * (p % 2), PAIRS * u + p, u % RING
                act.wait_ge(s_max, count(2 * PAIRS, u, i, 2 * (p + 1)))
                for z in range(2):
                    t = t0 + z
                    last = nc.scalar.activation(unused[:, n % 2, z, :], s_ps[:, n % 2, z, SMALL:TOK], ACT.Exp,
                                                bias=negmax[:, r, t, IP, j:j + 1],
                                                accum_out=sums[:, r, t, IP, j:j + 1])
                last.then_inc(s_exp, 1)

            def small_exp(u, h, i):
                act.wait_ge(sm_sub, count(4, u, i, 2 * (h + 1)))
                half = small[:, h * 8:(h + 1) * 8, :]
                nc.scalar.activation(half, half, ACT.Exp).then_inc(sm_exp, 1)

            def logs_of(u, i):
                act.wait_ge(sm_sum, count(4, u, i, 4))
                act.wait_ge(s_exp, count(PAIRS, u, i, PAIRS))
                if due(n_due := count(3, u, i)):
                    act.wait_ge(lse_step, n_due)
                nc.scalar.activation(logs[:, :, :, :], sums[:, u % RING, :, :, :], ACT.Ln).then_inc(ln_done, 1)

            def slot(m, i):
                for k in range(STEPS):
                    if k == 0 and there(m - 3, i):
                        logs_of(m - 3, i)
                    u, items = items_at(m, k)
                    if there(u, i):
                        prob(u, items, i)
                    if k == 0 and there(m - 1, i):
                        u = m - 1
                        act.wait_ge(q_acc, count(1, u, i, 1))
                        if not isinstance(i, int) or u > 0:
                            act.wait_ge(q_packed[(u - 1) % RING], 16 * len(BLOCKS) * HPU * use(u - 1, i))
                        nc.scalar.activation(q_out[:, HI, :], m_ps[:, :], ACT.Copy, scale=SCALE).then_inc(q_hi, 1)
                    u, p = pair_at(m, k)
                    if there(u, i):
                        ip_sums(u, p, i)
                    if k in (3, 7) and there(m - 2, i):
                        small_exp(m - 2, k // 4, i)
                    if k == 4 and there(m - 4, i):
                        u = m - 4
                        act.wait_ge(pv_done, count(KT, u, i, KT))
                        if due(n_due := count(QC, u - 1, i, 1)):
                            act.wait_ge(y_done, n_due)
                        nc.scalar.activation(heads[:, u % RING, HI, :], o_ps[:, :], ACT.Copy).then_inc(o_hi, 1)
                    if m % QC == 0 and k < QC and there(m, i):
                        if k == 0:
                            if due(n_due := count(1, m, i)):
                                act.wait_ge(q_acc, n_due)
                        split_hi(piece(m, i, k), i, xs[:, HI, k, :], TOK)

            in_slots(act, slot)

        @block.vector
        def _(dve):
            def split_lo(n, i, hi, lo, width):
                dve.wait_ge(x_hi, n + 1 + LOOP * i)
                nc.vector.tensor_tensor(lo, xraw[:, n % XR, 0:width], hi.bitcast(F32), ALU.subtract).then_inc(x_lo, 1)

            for z, w in enumerate((wq, wo)):
                for c in range(QC):
                    split_lo(z * QC + c, 0, w[:, HI, c, :], w[:, LO, c, :], CH)

            def pair_max(u, p, i):
                j, t0, n, r = p // 2, 2 * (p % 2), PAIRS * u + p, u % RING
                dve.wait_ge(s_done, count(PAIRS, u, i, p + 1))
                nc.vector.tensor_reduce(negmax[:, r, t0:t0 + 2, IP, j], s_ps[:, n % 2, :, SMALL:TOK], AX_X, ALU.max,
                                        negate=True).then_inc(s_max, 1)
                if p % (PAIRS // 2) == 0:
                    if due(n_due := count(4, u - 1, i, 2 + 2 * (p // (PAIRS // 2)))):
                        dve.wait_ge(sm_sum, n_due)
                w = j * QT + t0
                nc.vector.tensor_copy(small[:, w:w + 2, :], s_ps[:, n % 2, :, 0:SMALL]).then_inc(s_max, 1)

            def halves(h):
                s = small[:, h * 8:(h + 1) * 8, :]
                return (s[:, :, 0:N_TXT].rearrange("p (j t) n -> p j t n", t=QT),
                        s[:, :, N_TXT:SMALL].rearrange("p (j t) (g n) -> p j t g n", t=QT, g=2))

            def stat(tile, r, h):
                s = tile[:, r, :, :, 2 * h:2 * h + 2]
                return (s[:, :, 0, :].rearrange("p t j -> p j t"), s[:, :, 1:3, :].rearrange("p t g j -> p j t g"))

            def less_max(u, h, i):
                (txt, two), (m_txt, m_two) = halves(h), stat(negmax, u % RING, h)
                dve.wait_ge(s_max, count(2 * PAIRS, u, i, PAIRS * (h + 1)))
                nc.vector.tensor_reduce(m_txt, txt, AX_X, ALU.max, negate=True).then_inc(row_max, 1)
                for j in range(2):
                    last = nc.vector.tensor_reduce(m_two[:, j], two[:, j], AX_X, ALU.max, negate=True)
                last.then_inc(row_max, 1)
                dve.wait_ge(row_max, count(4, u, i, 2 * (h + 1)))
                nc.vector.tensor_tensor(txt, txt, m_txt.unsqueeze(3).to_broadcast([P, 2, QT, N_TXT]), ALU.add)\
                    .then_inc(sm_sub, 1)
                for j in range(2):
                    last = nc.vector.tensor_tensor(two[:, j], two[:, j],
                                                   m_two[:, j].unsqueeze(3).to_broadcast([P, QT, 2, N_OBJ]), ALU.add)
                last.then_inc(sm_sub, 1)

            def small_sums(u, h, i):
                (txt, two), (s_txt, s_two) = halves(h), stat(sums, u % RING, h)
                dve.wait_ge(sm_exp, count(2, u, i, h + 1))
                nc.vector.tensor_reduce(s_txt, txt, AX_X, ALU.add).then_inc(sm_sum, 1)
                for j in range(2):
                    last = nc.vector.tensor_reduce(s_two[:, j], two[:, j], AX_X, ALU.add)
                last.then_inc(sm_sum, 1)

            def lse_parts(u, i):
                if due(n_due := count(1, u, i)):
                    dve.wait_ge(lse_t, n_due)
                dve.wait_ge(ln_done, count(1, u, i, 1))
                nc.vector.tensor_tensor(neglse[:, :, :, :], negmax[:, u % RING, :, :, :], logs[:, :, :, :],
                                        ALU.subtract).then_inc(lse_step, 1)
                dve.wait_ge(lse_step, count(3, u, i, 1))
                nc.vector.tensor_copy(neglse2[:, :, HI, :, :], neglse[:, :, :, :]).then_inc(lse_step, 1)
                dve.wait_ge(lse_step, count(3, u, i, 2))
                nc.vector.tensor_tensor(neglse2[:, :, LO, :, :], neglse[:, :, :, :],
                                        neglse2[:, :, HI, :, :].bitcast(F32), ALU.subtract).then_inc(lse_step, 1)

            def lse_keep(u, i):
                dve.wait_ge(lse_t, count(1, u, i, 1))
                if not isinstance(i, int) or u > 0:
                    dve.wait_ge(lse_packed[(u - 1) % RING], 16 * use(u - 1, i))
                nc.vector.tensor_copy(lse_rows[:, :], m_ps[0:2 * GROUPS * HPU, :]).then_inc(lse_sb, 1)

            def add_output(u, i, c):
                dve.wait_ge(y_done, count(QC, u, i, c + 1))
                if u % QC == 0:
                    dve.wait_ge(res_in[c], 16 * (batch(u, i) + 1))
                    dve.wait_ge(const_in, 48)
                    nc.vector.scalar_tensor_tensor(out=acc[:, c, :], in0=m_ps[:, :], scalar=bias[:, c:c + 1],
                                                   in1=acc[:, c, :], op0=ALU.add, op1=ALU.add).then_inc(y_added, 1)
                else:
                    dve.wait_ge(y_added, count(QC, u - 1, i, c + 1))
                    nc.vector.tensor_tensor(acc[:, c, :], m_ps[:, :], acc[:, c, :], ALU.add).then_inc(y_added, 1)

            def slot(m, i):
                for k in range(STEPS):
                    u, p = pair_at(m, k)
                    if there(u, i):
                        pair_max(u, p, i)
                    if k == 0 and there(m - 3, i):
                        lse_parts(m - 3, i)
                    if k == 0 and there(m - 1, i):
                        dve.wait_ge(q_hi, count(1, m - 1, i, 1))
                        nc.vector.scalar_tensor_tensor(out=q_out[:, LO, :], in0=m_ps[:, :], scalar=SCALE,
                                                       in1=q_out[:, HI, :].bitcast(F32), op0=ALU.mult,
                                                       op1=ALU.subtract).then_inc(q_lo, 1)
                    if k == 1 and there(m - 3, i):
                        lse_keep(m - 3, i)
                    if k in Y_STEPS and there(m - 5, i):
                        add_output(m - 5, i, k - Y_STEPS[0])
                    if k in (2, 6) and there(m - 2, i):
                        less_max(m - 2, k // 4, i)
                    if k in (4, 7) and there(m - 2, i):
                        small_sums(m - 2, k // 6, i)
                    if k == 4 and there(m - 4, i):
                        u = m - 4
                        dve.wait_ge(o_hi, count(1, u, i, 1))
                        nc.vector.tensor_tensor(heads[:, u % RING, LO, :], o_ps[:, :],
                                                heads[:, u % RING, HI, :].bitcast(F32), ALU.subtract).then_inc(o_lo, 1)
                    if m % QC == 0 and k < QC and there(m, i):
                        split_lo(piece(m, i, k), i, xs[:, HI, k, :], xs[:, LO, k, :], TOK)

            in_slots(dve, slot)


WEIGHTS = {"k_txt": "to_k_w", "v_txt": "to_v_w", "k_obj": "to_k_object_w", "v_obj": "to_v_object_w",
           "k_oth": "to_k_others_w", "v_oth": "to_v_others_w", "k_ip": "to_k_ip_w", "v_ip": "to_v_ip_w",
           "wq": "to_q_w", "wo": "to_out_w"}


def build(nc, d):
    project_context(nc, d)
    attend(nc, d)


def kernel(**inputs):
    import numpy as _np
    import concourse.bacc as _bacc
    from concourse import mybir as _mybir
    from concourse.bass_utils import run_bass_kernel_spmd as _run

    x, context = _np.asarray(inputs["x"]), _np.asarray(inputs["ctx_2048"])
    host = {"xT": x.transpose(0, 2, 1), "ctxT": context.transpose(0, 2, 1)}
    by_channel = context.transpose(2, 0, 1)
    at = 0
    for g, n in (("txt", N_TXT), ("obj", N_OBJ), ("oth", N_OTH), ("rest", REST)):
        host[f"ctxT_{g}"] = by_channel[:, :, at:at + n].reshape(CTX, BATCH * n)
        at += n
    for name, source in WEIGHTS.items():
        host[name] = _np.asarray(inputs[f"L0_xattn_{source}"])
    host["bias"] = _np.asarray(inputs["L0_xattn_to_out_b"]).reshape(QC, P).T
    bounds = [0, N_TXT, N_TXT + N_OBJ, SMALL, TOK]
    rows = _np.zeros((2 * GROUPS, TOK), _np.float32)
    for g in range(GROUPS):
        rows[[g, GROUPS + g], bounds[g]:bounds[g + 1]] = 1
    host["group_rows"] = rows
    host["ident"] = _np.eye(P, dtype=_np.float32)

    nc = _bacc.Bacc("TRN2", target_bir_lowering=False, num_devices=1)
    arrays, d = {}, {}
    for name, a in host.items():
        arrays[f"in_{name}"] = _np.ascontiguousarray(a)
        d[name] = nc.dram_tensor(f"in_{name}", a.shape, F32, kind="ExternalInput").ap()
    d["kT"] = nc.dram_tensor("kT", (BATCH, 2, CH, TOK), F32, kind="Internal").ap()
    for g, n in (("txt", N_TXT), ("obj", N_OBJ), ("oth", N_OTH), ("rest", REST)):
        d[f"v_{g}_rows"] = nc.dram_tensor(f"v_{g}_rows", (BATCH * n, CH), F32, kind="Internal").ap()
    d["v_ip_rows"] = nc.dram_tensor("v_ip_rows", (BATCH, TOK - P, CH), F32, kind="Internal").ap()
    d["yT"] = nc.dram_tensor("out_yT", (BATCH, CH, TOK), F32, kind="ExternalOutput").ap()
    build(nc, d)
    r = _run(nc, [arrays], core_ids=[0])
    return _np.ascontiguousarray(r.results[0]["out_yT"].transpose(0, 2, 1))
```

```python
from contextlib import ExitStack

import concourse.bass as bass
from concourse import mybir

ALU = mybir.AluOpType
ACT = mybir.ActivationFunctionType
AX_X = mybir.AxisListType.X
F32 = mybir.dt.float32
F32R = mybir.dt.float32r
BF16 = mybir.dt.bfloat16

BATCH = 16
TOK = 512
CH = 640
CTX = 1024
HD = 32
P = 128
QC = CH // P
CC = CTX // P
HPU = P // HD
N_TXT, N_OBJ, N_OTH = 77, 4, 4
SMALL = N_TXT + N_OBJ + N_OTH
N_IP = TOK - SMALL
REST = P - SMALL
GROUPS = 4
SCALE = float(HD) ** -0.5

HI, LO = 0, 1
PASSES = ((HI, HI), (HI, LO), (LO, HI))

IPN = TOK - SMALL + 1
TXT_B = 4
REST_B = 8
N_TXT_RUNS = BATCH // TXT_B
N_REST_RUNS = BATCH // REST_B
RUN_OBJ = N_TXT_RUNS
RUN_OTH = RUN_OBJ + 1
RUN_REST = RUN_OTH + 1
RUN_IP = RUN_REST + N_REST_RUNS
RUNS = RUN_IP + BATCH
RAW = 4
WS = 3


def v_tiles(n):
    return [(a, min(P, n - a)) for a in range(0, n, P)]


def due(count):
    return not isinstance(count, int) or count > 0


def project_context(nc, d):
    with ExitStack() as ctx:
        def sb(name, shape, dt):
            return ctx.enter_context(nc.sbuf_tensor(name, shape, dt))

        def sem(name):
            return ctx.enter_context(nc.semaphore(name))

        w = sb("w_split", [P, WS, 2, CC, CH], F32R)
        c = sb("ctx_split", [P, 2, 2, CC, IPN], F32R)
        raw = sb("raw", [P, RAW, CH], F32)
        k_out = sb("k_out", [P, 2, 2, TOK], F32R)
        v_out = sb("v_out", [P, 2, CH], F32)
        k_ps = ctx.enter_context(nc.psum_tensor("k_ps", [P, 2, 512], F32))
        v_ps = ctx.enter_context(nc.psum_tensor("v_ps", [P, 2, 2, 512], F32))

        raw_in = [sem(f"raw_in{r}") for r in range(RAW)]
        piece_hi = sem("piece_hi")
        piece_lo = sem("piece_lo")
        k_acc = sem("k_acc")
        k_hi = sem("k_hi")
        k_lo = sem("k_lo")
        v_acc = sem("v_acc")
        v_sb = sem("v_sb")
        k_stored = [sem(f"k_stored{r}") for r in range(2)]
        v_stored = [sem(f"v_stored{r}") for r in range(2)]

        W_ORDER = [("k_txt", 0, -1), ("v_txt", 1, -1), ("k_obj", 2, 0), ("v_obj", 0, RUN_OBJ - 1),
                   ("k_oth", 1, RUN_OBJ - 1), ("v_oth", 2, RUN_OBJ), ("k_ip", 0, RUN_OBJ), ("v_ip", 1, RUN_OTH)]
        SLOT = {name: slot for name, slot, _ in W_ORDER}

        def group_of(run):
            return ("txt" if run < RUN_OBJ else "obj" if run < RUN_OTH else "oth" if run < RUN_REST else
                    "rest" if run < RUN_IP else "ip")

        def width(run):
            return {"txt": TXT_B * N_TXT, "obj": BATCH * N_OBJ, "oth": BATCH * N_OTH, "rest": REST_B * REST,
                    "ip": IPN}[group_of(run)]

        def k_blocks(run):
            return 0 if group_of(run) == "rest" else QC

        def tiles(run):
            if group_of(run) == "ip":
                return [(P * (t + 1) - SMALL + 1, P) for t in range(TOK // P - 1)]
            return v_tiles(width(run))

        k_base, v_base, lots = [0], [0], []
        for run in range(RUNS):
            k_base.append(k_base[-1] + k_blocks(run))
            v_base.append(v_base[-1] + len(tiles(run)))
        lots += [("w", "k_txt"), ("c", 0), ("w", "v_txt")]
        for run in range(RUNS - 1):
            lots += [("c", run + 1)] + [("w", name) for name, _, after in W_ORDER if after == run]
        LOT = {lot: n for n, lot in enumerate(lots)}

        def pieces_upto(kind, which):
            return CC * (LOT[(kind, which)] + 1)

        def ready(run):
            need = [pieces_upto("c", run)]
            g = "ip" if group_of(run) == "rest" else group_of(run)
            need += [pieces_upto("w", f"v_{g}")] + [pieces_upto("w", f"k_{g}")] * (k_blocks(run) > 0)
            return max(need)

        PER_TURN = 2
        TURNS = (BATCH - PER_TURN) // PER_TURN
        D_PIECE, D_K, D_V = PER_TURN * CC, PER_TURN * QC, PER_TURN * len(tiles(RUN_IP))

        def ctx_src(run0, i, n):
            g, rows = group_of(run0), slice(n * P, (n + 1) * P)
            if g == "ip":
                return d["ctxT"][run0 - RUN_IP + PER_TURN * i, rows, TOK - IPN:TOK]
            if g == "txt":
                return d["ctxT_txt"][rows, run0 * width(0):(run0 + 1) * width(0)]
            if g == "rest":
                return d["ctxT_rest"][rows, (run0 - RUN_REST) * width(run0):(run0 - RUN_REST + 1) * width(run0)]
            return d[f"ctxT_{g}"][rows, :]

        def in_turns(eng, one_run):
            for run in range(RUN_IP):
                one_run(run, 0)
            with eng.Fori(0, TURNS) as i:
                for run in range(RUN_IP, RUN_IP + PER_TURN):
                    one_run(run, i)
            for run in range(RUNS - PER_TURN, RUNS):
                one_run(run, 0)

        block = ctx.enter_context(nc.Block())

        @block.sync
        def _(sp):
            def load(k0, i, src):
                if due(n_due := k0 - RAW + 1 + D_PIECE * i):
                    sp.wait_ge(piece_lo, n_due)
                sp.dma_start(raw[:, k0 % RAW, 0:src.shape[-1]], src).then_inc(raw_in[k0 % RAW], 16)

            def load_w(name):
                for n in range(CC):
                    load(CC * LOT[("w", name)] + n, 0, d[name][n * P:(n + 1) * P, :])

            load_w("k_txt")
            for n in range(CC):
                load(CC * LOT[("c", 0)] + n, 0, ctx_src(0, 0, n))
            load_w("v_txt")

            def store_k(run0, i, m):
                k0, g, n = k_base[run0] + m, group_of(run0), width(run0)
                sp.wait_ge(k_lo, k0 + 1 + D_K * i)
                for part in (HI, LO):
                    rows = slice(m * P, (m + 1) * P)
                    if g == "ip":
                        dst = d["kT"][run0 - RUN_IP + PER_TURN * i, part, rows, SMALL:TOK]
                        src = k_out[:, k0 % 2, part, 1:n]
                    else:
                        at, size = {"txt": (0, N_TXT), "obj": (N_TXT, N_OBJ), "oth": (N_TXT + N_OBJ, N_OTH)}[g]
                        b0 = TXT_B * run0 if g == "txt" else 0
                        dst = d["kT"][b0:b0 + n // size, part, rows, at:at + size].rearrange("b p t -> p b t")
                        src = k_out[:, k0 % 2, part, 0:n].rearrange("p (b t) -> p b t", t=size)
                    sp.dma_start(dst, src.bitcast(F32)).then_inc(k_stored[k0 % 2], 16)

            def store_v(run0, i, t):
                v0, g, (a, rows) = v_base[run0] + t, group_of(run0), tiles(run0)[t]
                if g == "ip":
                    dst = d["v_ip_rows"][run0 - RUN_IP + PER_TURN * i, t * P:(t + 1) * P, :]
                else:
                    a += {"txt": run0, "rest": run0 - RUN_REST}.get(g, 0) * width(run0)
                    dst = d[f"v_{g}_rows"][a:a + rows, :]
                sp.wait_ge(v_sb, v0 + 1 + D_V * i)
                sp.dma_start(dst, v_out[0:rows, v0 % 2, :]).then_inc(v_stored[v0 % 2], 16)

            def one_run(run0, i):
                blocks = k_blocks(run0)
                for n in range(CC):
                    if run0 < RUNS - 1:
                        load(CC * LOT[("c", run0 + 1)] + n, i, ctx_src(run0 + 1, i, n))
                    if n < blocks:
                        store_k(run0, i, n)
                    elif n - blocks < len(tiles(run0)):
                        store_v(run0, i, n - blocks)
                for name, _, after in W_ORDER:
                    if after == run0:
                        load_w(name)

            in_turns(sp, one_run)
            for r in range(2):
                sp.wait_ge(k_stored[r], 32 * ((k_base[RUNS] - r + 1) // 2))
                sp.wait_ge(v_stored[r], 16 * ((v_base[RUNS] - r + 1) // 2))

        @block.scalar
        def _(act):
            def split_hi(k0, i, dst, n):
                act.wait_ge(raw_in[k0 % RAW], 16 * (k0 // RAW + 1) + 16 * (D_PIECE // RAW) * i)
                nc.scalar.activation(dst, raw[:, k0 % RAW, 0:n], ACT.Copy).then_inc(piece_hi, 1)

            def split_ctx(run0, i, n):
                if n == 0:
                    if due(n_due := v_base[max(run0 - 1, 0)] + D_V * i):
                        act.wait_ge(v_acc, n_due)
                split_hi(CC * LOT[("c", run0)] + n, i, c[:, run0 % 2, HI, n, 0:width(run0)], width(run0))

            def split_w(name, after):
                if due(n_due := v_base[after + 1]):
                    act.wait_ge(v_acc, n_due)
                for n in range(CC):
                    split_hi(CC * LOT[("w", name)] + n, 0, w[:, SLOT[name], HI, n, :], CH)

            split_w("k_txt", -1)
            for n in range(CC):
                split_ctx(0, 0, n)
            split_w("v_txt", -1)

            def keep_k(run0, i, m):
                k0, n = k_base[run0] + m, width(run0)
                act.wait_ge(k_acc, k0 + 1 + D_K * i)
                if due(n_due := 32 * (k0 // 2) + 16 * D_K * i):
                    act.wait_ge(k_stored[k0 % 2], n_due)
                nc.scalar.activation(k_out[:, k0 % 2, HI, 0:n], k_ps[:, k0 % 2, 0:n], ACT.Copy).then_inc(k_hi, 1)

            def keep_v(run0, i, t):
                v0, rows = v_base[run0] + t, tiles(run0)[t][1]
                act.wait_ge(v_acc, v0 + 1 + D_V * i)
                if due(n_due := 16 * (v0 // 2) + 8 * D_V * i):
                    act.wait_ge(v_stored[v0 % 2], n_due)
                nc.scalar.activation(v_out[0:rows, v0 % 2, :].rearrange("p (a n) -> p a n", a=2),
                                     v_ps[0:rows, v0 % 2, :, 0:CH // 2], ACT.Copy).then_inc(v_sb, 1)

            def one_run(run0, i):
                blocks = k_blocks(run0)
                for n in range(CC):
                    if run0 < RUNS - 1:
                        split_ctx(run0 + 1, i, n)
                    if n < blocks:
                        keep_k(run0, i, n)
                    elif n - blocks < len(tiles(run0)):
                        keep_v(run0, i, n - blocks)
                for name, _, after in W_ORDER:
                    if after == run0:
                        split_w(name, after)

            in_turns(act, one_run)

        @block.vector
        def _(dve):
            def split_lo(k0, i, hi, lo, n):
                dve.wait_ge(piece_hi, k0 + 1 + D_PIECE * i)
                nc.vector.tensor_tensor(lo, raw[:, k0 % RAW, 0:n], hi.bitcast(F32), ALU.subtract).then_inc(piece_lo, 1)

            def split_ctx(run0, i, n):
                b, wd = run0 % 2, width(run0)
                split_lo(CC * LOT[("c", run0)] + n, i, c[:, b, HI, n, 0:wd], c[:, b, LO, n, 0:wd], wd)

            def split_w(name):
                s = SLOT[name]
                for n in range(CC):
                    split_lo(CC * LOT[("w", name)] + n, 0, w[:, s, HI, n, :], w[:, s, LO, n, :], CH)

            split_w("k_txt")
            for n in range(CC):
                split_ctx(0, 0, n)
            split_w("v_txt")

            def keep_k(run0, i, m):
                k0, n = k_base[run0] + m, width(run0)
                dve.wait_ge(k_hi, k0 + 1 + D_K * i)
                nc.vector.tensor_tensor(k_out[:, k0 % 2, LO, 0:n], k_ps[:, k0 % 2, 0:n],
                                        k_out[:, k0 % 2, HI, 0:n].bitcast(F32), ALU.subtract).then_inc(k_lo, 1)

            def one_run(run0, i):
                for n in range(CC):
                    if run0 < RUNS - 1:
                        split_ctx(run0 + 1, i, n)
                    if n < k_blocks(run0):
                        keep_k(run0, i, n)
                for name, _, after in W_ORDER:
                    if after == run0:
                        split_w(name)

            in_turns(dve, one_run)

        @block.tensor
        def _(pe):
            def one_run(run0, i):
                g, n, b = group_of(run0), width(run0), run0 % 2
                wg = "ip" if g == "rest" else g
                pe.wait_ge(piece_lo, ready(run0) + D_PIECE * i)
                for m in range(k_blocks(run0)):
                    k0, s = k_base[run0] + m, SLOT[f"k_{wg}"]
                    if due(n_due := k0 - 1 + D_K * i):
                        pe.wait_ge(k_lo, n_due)
                    for q in range(CC):
                        for z, (pw, px) in enumerate(PASSES):
                            last = nc.tensor.matmul(k_ps[:, k0 % 2, 0:n], w[:, s, pw, q, m * P:(m + 1) * P],
                                                    c[:, b, px, q, 0:n], start=(q == 0 and z == 0),
                                                    stop=(q == CC - 1 and z == len(PASSES) - 1))
                    last.then_inc(k_acc, 1)
                s = SLOT[f"v_{wg}"]
                for t, (a, rows) in enumerate(tiles(run0)):
                    v0 = v_base[run0] + t
                    if due(n_due := v0 - 1 + D_V * i):
                        pe.wait_ge(v_sb, n_due)
                    for half in range(2):
                        for q in range(CC):
                            for z, (px, pw) in enumerate(PASSES):
                                last = nc.tensor.matmul(
                                    v_ps[0:rows, v0 % 2, half, 0:CH // 2], c[:, b, px, q, a:a + rows],
                                    w[:, s, pw, q, half * (CH // 2):(half + 1) * (CH // 2)],
                                    start=(q == 0 and z == 0), stop=(q == CC - 1 and z == len(PASSES) - 1))
                    last.then_inc(v_acc, 1)

            in_turns(pe, one_run)


UNITS = BATCH * QC
RING = 3
LOOP = RING * QC
STEPS = 8
QT = TOK // P
KT = TOK // P
PAIRS = HPU * QT // 2
ITEMS = HPU * KT
PR = 6
XR = 5
HR = 2 * QC
W_COLS = CH // 2
ROWS_S = 3 * HD
ROWS_ST = ROWS_S + 2 * GROUPS
BLOCKS = ((HI, HI), (LO, HI), (HI, LO))
IP = GROUPS - 1
PARTS = ((0, HPU // 2), (HPU // 2, HPU))
PAIRS_UPTO = [2 * to for _, to in PARTS]
Q_PRODUCTS = {6: (0, 4), 7: (4, 10)}
Y_LAG = 9
Y_PRODUCTS = {2: (0, 4), 3: (4, 8), 4: (8, 12), 5: (12, 15)}


def attend(nc, d):
    with ExitStack() as ctx:
        def sb(name, shape, dt):
            return ctx.enter_context(nc.sbuf_tensor(name, shape, dt))

        def psum(name, shape):
            return ctx.enter_context(nc.psum_tensor(name, shape, F32))

        def sem(name):
            return ctx.enter_context(nc.semaphore(name))

        wq = sb("wq", [P, 2, QC, CH], F32R)
        wo = sb("wo", [P, 2, QC, CH], F32R)
        xraw = sb("xraw", [P, XR, TOK], F32)
        xs = sb("xs", [P, 2, QC, TOK], F32R)
        q_out = sb("q_out", [P, 2, TOK], F32R)
        qpack = sb("qpack", [P, RING, HPU, TOK], F32R)
        kpack = sb("kpack", [P, RING, HPU, TOK], F32R)
        vt = sb("vt", [P, RING, KT, P], F32)
        small = sb("small", [P, HPU * QT, SMALL], F32)
        negmax = sb("negmax", [P, RING, GROUPS, HPU, QT], F32)
        sums = sb("sums", [P, RING, GROUPS, HPU, QT], F32)
        logs = sb("logs", [P, GROUPS, HPU, QT], F32)
        neglse = sb("neglse", [P, GROUPS, HPU, QT], F32)
        neglse2 = sb("neglse2", [P, 2, GROUPS, HPU, QT], F32R)
        lse_rows = sb("lse_rows", [2 * GROUPS * HPU, TOK], F32R)
        probs = sb("probs", [P, PR, TOK], F32)
        heads = sb("heads", [P, HR, 2, TOK], F32R)
        out = sb("out", [P, RING, TOK], F32)
        ident = sb("ident", [P, P], F32)
        bias = sb("bias", [P, QC], F32)

        s_ps = psum("s_ps", [P, 2, 2, 512])
        st_ps = psum("st_ps", [P, 2, 512])
        o_ps = psum("o_ps", [P, 512])
        m_ps = psum("m_ps", [P, 512])

        const_in = sem("const_in")
        raw_in = [sem(f"raw2_in{r}") for r in range(XR)]
        x_hi, x_lo = sem("x_hi"), sem("x_lo")
        rows_set = sem("rows_set")
        q_acc, q_hi, q_lo = sem("q_acc"), sem("q_hi"), sem("q_lo")
        q_packed = [sem(f"q_packed{r}") for r in range(RING)]
        k_packed = [sem(f"k_packed{r}") for r in range(RING)]
        v_in = [sem(f"v_in{r}") for r in range(RING)]
        s_done = sem("s_done")
        s_max = sem("s_max")
        s_exp = sem("s_exp")
        row_max = sem("row_max")
        sm_sub = sem("sm_sub")
        sm_exp = sem("sm_exp")
        sm_sum = sem("sm_sum")
        ln_done = sem("ln_done")
        lse_step = sem("lse_step")
        lse_t = sem("lse_t")
        lse_sb = sem("lse_sb")
        lse_packed = [sem(f"lse_packed{r}") for r in range(RING)]
        st_done = sem("st_done")
        p_done = sem("p_done")
        pv_done = sem("pv_done")
        o_hi, o_lo = sem("o_hi"), sem("o_lo")
        y_done = sem("y_done")
        y_added = sem("y_added")
        res_in = [sem(f"res_in{r}") for r in range(RING)]
        y_out = [sem(f"y_out{r}") for r in range(RING)]

        def count(per, k, i, more=0):
            return per * k + more + per * LOOP * i

        def use(k, i):
            return k // RING + 1 + (LOOP // RING) * i

        def batch(k, i):
            return k // QC + (LOOP // QC) * i

        def there(k, i):
            return 0 <= k < UNITS if isinstance(i, int) else True

        PRELUDE = 20
        TURNS = (UNITS - PRELUDE) // LOOP
        assert PRELUDE >= Y_LAG and PRELUDE + TURNS * LOOP == UNITS and TURNS % 2 == 0
        assert LOOP % RING == 0 and LOOP * ITEMS % PR == 0 and LOOP % XR == 0 and 2 * LOOP % HR == 0

        def in_slots(eng, slot, at_once=1):
            for m in range(PRELUDE):
                slot(m, 0)
            with eng.Fori(0, TURNS, at_once) as i:
                for m in range(PRELUDE, PRELUDE + at_once * LOOP):
                    slot(m, i)
            for m in range(UNITS, UNITS + Y_LAG):
                slot(m, 0)

        def pair_at(m, k):
            return (m - 1, k - 6) if k >= 6 else (m - 2, k + 2)

        def items_at(m, k):
            u, at = (m - 3, k - 3) if k >= 3 else (m - 4, k + 5)
            return u, (2 * at, 2 * at + 1)

        def small_groups(h):
            s = small[:, QT * PARTS[h][0]:QT * PARTS[h][1], :]
            return s[:, :, 0:N_TXT], s[:, :, N_TXT:SMALL].rearrange("p w (g n) -> p w g n", g=2)

        def small_stats(tile, u, h):
            s = tile[:, u % RING, :, PARTS[h][0]:PARTS[h][1], :].rearrange("p g j t -> p (j t) g")
            return s[:, :, 0], s[:, :, 1:IP]

        def over_keys(stats, n):
            dims = len(stats.shape)
            return stats.unsqueeze(dims).to_broadcast([*stats.shape, n])

        small_rows = small[ROWS_S:ROWS_ST, :, :].rearrange("p w n -> p (w n)")[:, 0:TOK]

        def weight_pieces():
            n = 0
            for z in range(2):
                for c in range(QC):
                    for at in range(0, CH, W_COLS):
                        yield n, z, c, slice(at, at + W_COLS)
                        n += 1

        PIECES_W = 2 * QC * (CH // W_COLS)

        def piece(k, i, c):
            return PIECES_W + k + c

        block = ctx.enter_context(nc.Block())

        @block.sync
        def _(sp):
            sp.dma_start(ident[:, :], d["ident"]).then_inc(const_in, 16)
            sp.dma_start(bias[:, :], d["bias"]).then_inc(const_in, 16)
            sp.dma_start(small_rows, d["group_rows"]).then_inc(const_in, 16)

            def load(n, i, src):
                if due(n_due := n - XR + 1 + LOOP * i):
                    sp.wait_ge(x_lo, n_due)
                sp.dma_start(xraw[:, n % XR, 0:src.shape[-1]], src).then_inc(raw_in[n % XR], 16)

            for n, z, c, cols in weight_pieces():
                load(n, 0, d[("wq", "wo")[z]][c * P:(c + 1) * P, cols])

            def pack_keys(u, i):
                r, b, cols = u % RING, batch(u, i), slice(u % QC * P, (u % QC + 1) * P)
                if due(n_due := count(ITEMS, u - RING + 1, i)):
                    sp.wait_ge(st_done, n_due)
                for n, (_, part) in enumerate(BLOCKS):
                    sp.dma_start(kpack[n * HD:(n + 1) * HD, r, :, :].bitcast(F32),
                                 d["kT"][b, part, cols, :].rearrange("(j c) t -> c j t", c=HD)).then_inc(k_packed[r], 16)

            def pack_queries(u, i):
                r = u % RING
                sp.wait_ge(q_lo, count(1, u, i, 1))
                for n, (part, _) in enumerate(BLOCKS):
                    sp.dma_start(qpack[n * HD:(n + 1) * HD, r, :, :].bitcast(F32), q_out[:, part, :].bitcast(F32)).then_inc(q_packed[r], 16)

            def load_values(u, i):
                r, b, cols = u % RING, batch(u, i), slice(u % QC * P, (u % QC + 1) * P)
                if due(n_due := count(KT, u - RING + 1, i)):
                    sp.wait_ge(pv_done, n_due)
                row = 0
                for g, n in (("txt", N_TXT), ("obj", N_OBJ), ("oth", N_OTH), ("rest", REST)):
                    sp.dma_start(vt[row:row + n, r, 0, :], d[f"v_{g}_rows"][bass.ds(b * n, n), cols]).then_inc(v_in[r], 16)
                    row += n
                sp.dma_start(vt[:, r, 1:KT, :], d["v_ip_rows"][b, :, cols].rearrange("(t p) n -> p t n", p=P))\
                    .then_inc(v_in[r], 16)

            def rows_of(w, i):
                return batch(w, i), slice(w % QC * P, (w % QC + 1) * P)

            def slot(m, i):
                if m % QC == 0 and there(m, i):
                    for c in range(QC):
                        load(piece(m, i, c), i, d["xT"][batch(m, i), c * P:(c + 1) * P, :])
                w = m - Y_LAG - 1
                if there(w, i):
                    b, rows = rows_of(w, i)
                    sp.wait_ge(y_added, count(1, w, i, 1))
                    sp.dma_start(d["yT"][b, rows, :], out[:, w % RING, :]).then_inc(y_out[w % RING], 16)
                w = m - Y_LAG
                if there(w, i):
                    b, rows = rows_of(w, i)
                    if due(n_due := 16 * (use(w, i) - 1)):
                        sp.wait_ge(y_out[w % RING], n_due)
                    sp.dma_start(out[:, w % RING, :], d["xT"][b, rows, :]).then_inc(res_in[w % RING], 16)
                if there(m - 2, i):
                    load_values(m - 2, i)
                u = m - 3
                if there(u, i):
                    sp.wait_ge(lse_sb, count(1, u, i, 1))
                    sp.dma_start(qpack[ROWS_S:ROWS_ST, u % RING, :, :].bitcast(F32), lse_rows[:, :].bitcast(F32)).then_inc(lse_packed[u % RING], 16)
                if there(m - 1, i):
                    pack_keys(m - 1, i)
                    pack_queries(m - 1, i)

            in_slots(sp, slot)
            w = UNITS - 1
            b, rows = rows_of(w, 0)
            sp.wait_ge(y_added, UNITS)
            sp.dma_start(d["yT"][b, rows, :], out[:, w % RING, :]).then_inc(y_out[w % RING], 16)
            for r in range(RING):
                sp.wait_ge(y_out[r], 16 * len(range(r, UNITS, RING)))

        @block.gpsimd
        def _(pool):
            pool.wait_ge(const_in, 48)
            for r in range(RING):
                for j in range(HPU):
                    nc.gpsimd.tensor_copy(kpack[ROWS_S:ROWS_ST, r, j, :], small_rows).then_inc(rows_set, 1)

            def split_lo(n, i, hi, lo):
                pool.wait_ge(x_hi, n + 1 + LOOP * i)
                nc.gpsimd.tensor_tensor(lo, xraw[:, n % XR, 0:TOK], hi.bitcast(F32), ALU.subtract).then_inc(x_lo, 1)

            def less_max(u, i):
                txt, two = small_groups(0)
                m_txt, m_two = small_stats(negmax, u, 0)
                pool.wait_ge(row_max, count(4, u, i, 2))
                nc.gpsimd.tensor_tensor(txt, txt, over_keys(m_txt, N_TXT), ALU.add).then_inc(sm_sub, 1)
                nc.gpsimd.tensor_tensor(two, two, over_keys(m_two, N_OBJ), ALU.add).then_inc(sm_sub, 1)

            def slot(m, i):
                if m == 0:
                    pool.wait_ge(x_lo, PIECES_W)
                    pool.wait_ge(rows_set, RING * HPU)
                for k in range(STEPS):
                    if m % QC == 0 and k < QC and there(m, i):
                        split_lo(piece(m, i, k), i, xs[:, HI, k, :], xs[:, LO, k, :])
                    if k == 2 and there(m - 2, i):
                        less_max(m - 2, i)

            in_slots(pool, slot)

        @block.tensor
        def _(pe):
            pe.wait_ge(const_in, 48)
            pe.wait_ge(rows_set, RING * HPU)

            def scores(u, p, i):
                j, t0, n = p // 2, 2 * (p % 2), PAIRS * u + p
                if p == 0:
                    pe.wait_ge(q_packed[u % RING], 16 * len(BLOCKS) * use(u, i))
                    pe.wait_ge(k_packed[u % RING], 16 * len(BLOCKS) * use(u, i))
                if due(n_due := count(PAIRS, u, i, p - 1)):
                    pe.wait_ge(s_exp, n_due)
                for z in range(2):
                    t = t0 + z
                    last = nc.tensor.matmul(s_ps[:, n % 2, z, :], qpack[0:ROWS_S, u % RING, j, t * P:(t + 1) * P],
                                            kpack[0:ROWS_S, u % RING, j, :], start=True, stop=True)
                last.then_inc(s_done, 1)

            def scores_t(u, items, i):
                r = u % RING
                if items[0] == 0:
                    pe.wait_ge(lse_packed[r], 16 * use(u, i))
                for x in items:
                    kt, j = x // HPU, x % HPU
                    if due(n_due := count(ITEMS, u, i, x - 1)):
                        pe.wait_ge(p_done, n_due)
                    nc.tensor.matmul(st_ps[:, x % 2, :], kpack[0:ROWS_ST, r, j, kt * P:(kt + 1) * P],
                                     qpack[0:ROWS_ST, r, j, :], start=True, stop=True).then_inc(st_done, 1)

            def values(u, kt, i):
                r = u % RING
                if kt == 0:
                    pe.wait_ge(v_in[r], 16 * 5 * use(u, i))
                    if due(n_due := count(1, u, i)):
                        pe.wait_ge(o_lo, n_due)
                pe.wait_ge(p_done, count(ITEMS, u, i, HPU * (kt + 1)))
                for j in range(HPU):
                    last = nc.tensor.matmul(o_ps[j * HD:(j + 1) * HD, :], vt[:, r, kt, j * HD:(j + 1) * HD],
                                            probs[:, (ITEMS * u + HPU * kt + j) % PR, :], start=(kt == 0), stop=(kt == KT - 1))
                last.then_inc(pv_done, 1)

            def queries(u, i, products):
                if products[0] == 0:
                    if there(u - Y_LAG, i):
                        pe.wait_ge(y_added, count(1, u - Y_LAG, i, 1))
                    else:
                        if due(n_due := count(1, u - 2, i)):
                            pe.wait_ge(lse_sb, n_due)
                    pe.wait_ge(x_lo, piece(u // QC * QC, i, QC) + LOOP * i)
                cols = slice(u % QC * P, (u % QC + 1) * P)
                for n in products:
                    c, (pw, px) = n // len(PASSES), PASSES[n % len(PASSES)]
                    last = nc.tensor.matmul(m_ps[:, :], wq[:, pw, c, cols], xs[:, px, c, :], start=(n == 0),
                                            stop=(n == QC * len(PASSES) - 1))
                if products[-1] == QC * len(PASSES) - 1:
                    last.then_inc(q_acc, 1)

            def transpose_lse(u, i):
                pe.wait_ge(q_lo, count(1, u, i, 3) if there(u + 2, i) else UNITS)
                if not there(u + 2, i):
                    pe.wait_ge(y_added, count(1, u + 3 - Y_LAG, i))
                pe.wait_ge(lse_step, count(3, u, i, 3))
                for t in range(QT):
                    last = nc.tensor.transpose(m_ps[0:2 * GROUPS * HPU, t * P:(t + 1) * P],
                                               neglse2[:, :, :, :, t].bitcast(F32).rearrange("p a g j -> p (a g j)"),
                                               ident[:, :])
                last.then_inc(lse_t, 1)

            def output(w, i, products):
                if products[0] == 0:
                    pe.wait_ge(o_lo, count(1, w // QC * QC, i, QC))
                    if there(w + Y_LAG - 3, i):
                        pe.wait_ge(lse_sb, count(1, w + Y_LAG - 3, i, 1))
                    else:
                        pe.wait_ge(y_added, count(1, w, i))
                cols = slice(w % QC * P, (w % QC + 1) * P)
                for n in products:
                    z, (pw, po) = n // len(PASSES), PASSES[n % len(PASSES)]
                    last = nc.tensor.matmul(m_ps[:, :], wo[:, pw, z, cols], heads[:, (w // QC * QC + z) % HR, po, :],
                                            start=(n == 0), stop=(n == QC * len(PASSES) - 1))
                if products[-1] == QC * len(PASSES) - 1:
                    last.then_inc(y_done, 1)

            def slot(m, i):
                for k in range(STEPS):
                    u, p = pair_at(m, k)
                    if there(u, i):
                        scores(u, p, i)
                    u, items = items_at(m, k)
                    if there(u, i):
                        scores_t(u, items, i)
                    if k == 0 and there(m - 1, i):
                        queries(m - 1, i, range(Q_PRODUCTS[STEPS - 1][1], QC * len(PASSES)))
                    if k == 1 and there(m - 3, i):
                        transpose_lse(m - 3, i)
                    if k in Y_PRODUCTS and there(m - Y_LAG, i):
                        output(m - Y_LAG, i, range(*Y_PRODUCTS[k]))
                    if k in Q_PRODUCTS and there(m, i):
                        queries(m, i, range(*Q_PRODUCTS[k]))
                    for at, lag, kt in ((5, 3, 0), (7, 3, 1), (1, 4, 2), (3, 4, 3)):
                        if k == at and there(m - lag, i):
                            values(m - lag, kt, i)

            in_slots(pe, slot, 2)

        @block.scalar
        def _(act):
            def split_hi(n, i, dst, width):
                act.wait_ge(raw_in[n % XR], 16 * (n // XR + 1) + 16 * (LOOP // XR) * i)
                nc.scalar.activation(dst, xraw[:, n % XR, 0:width], ACT.Copy).then_inc(x_hi, 1)

            nc.scalar.preload_act_table_set("natural_log_exp_and_others")
            for n, z, c, cols in weight_pieces():
                split_hi(n, 0, (wq, wo)[z][:, HI, c, cols], W_COLS)

            def prob(u, items, i):
                for x in items:
                    act.wait_ge(st_done, count(ITEMS, u, i, x + 1))
                    if x % 2 == 0:
                        if due(n_due := count(KT, u, i, (x + 1 - PR) // HPU + 1)):
                            act.wait_ge(pv_done, n_due)
                    nc.scalar.activation(probs[:, (ITEMS * u + x) % PR, :], st_ps[:, x % 2, :], ACT.Exp).then_inc(p_done, 1)

            def ip_sums(u, p, i):
                j, t0, n, r = p // 2, 2 * (p % 2), PAIRS * u + p, u % RING
                act.wait_ge(s_max, count(2 * PAIRS, u, i, 2 * (p + 1)))
                for z in range(2):
                    t = t0 + z
                    last = nc.scalar.activation(s_ps[:, n % 2, z, SMALL:TOK], s_ps[:, n % 2, z, SMALL:TOK], ACT.Exp,
                                                bias=negmax[:, r, IP, j, t:t + 1],
                                                accum_out=sums[:, r, IP, j, t:t + 1])
                last.then_inc(s_exp, 1)

            def small_exp(u, h, i):
                act.wait_ge(sm_sub, count(4, u, i, 2 * (h + 1)))
                part = small[:, QT * PARTS[h][0]:QT * PARTS[h][1], :]
                nc.scalar.activation(part, part, ACT.Exp).then_inc(sm_exp, 1)

            def logs_of(u, i):
                act.wait_ge(sm_sum, count(4, u, i, 4))
                act.wait_ge(s_exp, count(PAIRS, u, i, PAIRS))
                if due(n_due := count(3, u, i)):
                    act.wait_ge(lse_step, n_due)
                nc.scalar.activation(logs[:, :, :, :], sums[:, u % RING, :, :, :], ACT.Ln).then_inc(ln_done, 1)

            def slot(m, i):
                for k in range(STEPS):
                    u, items = items_at(m, k)
                    if there(u, i):
                        prob(u, items, i)
                    if k == 0 and there(m - 3, i):
                        logs_of(m - 3, i)
                    if k == 6 and there(m - 2, i):
                        small_exp(m - 2, 1, i)
                    u, p = pair_at(m, k)
                    if there(u, i):
                        ip_sums(u, p, i)
                    if k == 3 and there(m - 2, i):
                        small_exp(m - 2, 0, i)

            in_slots(act, slot)

        @block.vector
        def _(dve):
            def split_lo(n, i, hi, lo, width):
                dve.wait_ge(x_hi, n + 1 + LOOP * i)
                nc.vector.tensor_tensor(lo, xraw[:, n % XR, 0:width], hi.bitcast(F32), ALU.subtract).then_inc(x_lo, 1)

            for n, z, c, cols in weight_pieces():
                split_lo(n, 0, (wq, wo)[z][:, HI, c, cols], (wq, wo)[z][:, LO, c, cols], W_COLS)

            def pair_max(u, p, i):
                j, t0, n, r = p // 2, 2 * (p % 2), PAIRS * u + p, u % RING
                dve.wait_ge(s_done, count(PAIRS, u, i, p + 1))
                nc.vector.tensor_reduce(negmax[:, r, IP, j, t0:t0 + 2], s_ps[:, n % 2, :, SMALL:TOK], AX_X, ALU.max,
                                        negate=True).then_inc(s_max, 1)
                if u == 0 and p == 0:
                    dve.wait_ge(rows_set, RING * HPU)
                for h, (first, _) in enumerate(PARTS):
                    if p == 2 * first:
                        if due(n_due := count(4, u - 1, i, 2 + 2 * h)):
                            dve.wait_ge(sm_sum, n_due)
                w = j * QT + t0
                nc.vector.tensor_copy(small[:, w:w + 2, :], s_ps[:, n % 2, :, 0:SMALL]).then_inc(s_max, 1)

            def small_max(u, h, i):
                txt, two = small_groups(h)
                m_txt, m_two = small_stats(negmax, u, h)
                dve.wait_ge(s_max, count(2 * PAIRS, u, i, 2 * PAIRS_UPTO[h]))
                nc.vector.tensor_reduce(m_txt, txt, AX_X, ALU.max, negate=True).then_inc(row_max, 1)
                nc.vector.tensor_reduce(m_two, two, AX_X, ALU.max, negate=True).then_inc(row_max, 1)

            def less_max(u, i):
                txt, two = small_groups(1)
                m_txt, m_two = small_stats(negmax, u, 1)
                dve.wait_ge(row_max, count(4, u, i, 4))
                nc.vector.tensor_tensor(txt, txt, over_keys(m_txt, N_TXT), ALU.add).then_inc(sm_sub, 1)
                nc.vector.tensor_tensor(two, two, over_keys(m_two, N_OBJ), ALU.add).then_inc(sm_sub, 1)

            def small_sums(u, h, i):
                txt, two = small_groups(h)
                s_txt, s_two = small_stats(sums, u, h)
                dve.wait_ge(sm_exp, count(2, u, i, h + 1))
                nc.vector.tensor_reduce(s_txt, txt, AX_X, ALU.add).then_inc(sm_sum, 1)
                nc.vector.tensor_reduce(s_two, two, AX_X, ALU.add).then_inc(sm_sum, 1)

            def lse_part(u, i, part):
                if part == 0:
                    if due(n_due := count(1, u, i)):
                        dve.wait_ge(lse_t, n_due)
                    dve.wait_ge(ln_done, count(1, u, i, 1))
                    nc.vector.tensor_tensor(neglse[:, :, :, :], negmax[:, u % RING, :, :, :], logs[:, :, :, :],
                                            ALU.subtract).then_inc(lse_step, 1)
                else:
                    dve.wait_ge(lse_step, count(3, u, i, part))
                if part == 1:
                    nc.vector.tensor_copy(neglse2[:, HI, :, :, :], neglse[:, :, :, :]).then_inc(lse_step, 1)
                elif part == 2:
                    nc.vector.tensor_tensor(neglse2[:, LO, :, :, :], neglse[:, :, :, :],
                                            neglse2[:, HI, :, :, :].bitcast(F32), ALU.subtract).then_inc(lse_step, 1)

            def queries_hi(u, i):
                dve.wait_ge(q_acc, count(1, u, i, 1))
                if not isinstance(i, int) or u > 0:
                    dve.wait_ge(q_packed[(u - 1) % RING], 16 * len(BLOCKS) * use(u - 1, i))
                nc.vector.tensor_scalar(q_out[:, HI, :], m_ps[:, :], SCALE, None, ALU.mult).then_inc(q_hi, 1)

            def queries_lo(u, i):
                dve.wait_ge(q_hi, count(1, u, i, 1))
                nc.vector.scalar_tensor_tensor(out=q_out[:, LO, :], in0=m_ps[:, :], scalar=SCALE,
                                               in1=q_out[:, HI, :].bitcast(F32), op0=ALU.mult,
                                               op1=ALU.subtract).then_inc(q_lo, 1)

            def heads_hi(u, i):
                dve.wait_ge(pv_done, count(KT, u, i, KT))
                if due(n_due := count(1, u // QC * QC, i, -QC)):
                    dve.wait_ge(y_done, n_due)
                nc.vector.tensor_copy(heads[:, u % HR, HI, :], o_ps[:, :]).then_inc(o_hi, 1)

            def heads_lo(u, i):
                dve.wait_ge(o_hi, count(1, u, i, 1))
                nc.vector.tensor_tensor(heads[:, u % HR, LO, :], o_ps[:, :], heads[:, u % HR, HI, :].bitcast(F32),
                                        ALU.subtract).then_inc(o_lo, 1)

            def split_hi(n, i, dst):
                dve.wait_ge(raw_in[n % XR], 16 * (n // XR + 1) + 16 * (LOOP // XR) * i)
                nc.vector.tensor_copy(dst, xraw[:, n % XR, :]).then_inc(x_hi, 1)

            def lse_keep(u, i):
                dve.wait_ge(lse_t, count(1, u, i, 1))
                if not isinstance(i, int) or u > 0:
                    dve.wait_ge(lse_packed[(u - 1) % RING], 16 * use(u - 1, i))
                nc.vector.tensor_copy(lse_rows[:, :], m_ps[0:2 * GROUPS * HPU, :]).then_inc(lse_sb, 1)

            def add_output(w, i):
                dve.wait_ge(y_done, count(1, w, i, 1))
                dve.wait_ge(res_in[w % RING], 16 * use(w, i))
                nc.vector.scalar_tensor_tensor(out=out[:, w % RING, :], in0=m_ps[:, :],
                                               scalar=bias[:, w % QC:w % QC + 1], in1=out[:, w % RING, :],
                                               op0=ALU.add, op1=ALU.add).then_inc(y_added, 1)

            def slot(m, i):
                for k in range(STEPS):
                    u, p = pair_at(m, k)
                    if there(u, i):
                        pair_max(u, p, i)
                    if k == 0:
                        if there(m - 3, i):
                            lse_part(m - 3, i, 0)
                        if there(m - 1, i):
                            queries_hi(m - 1, i)
                        if there(m - 3, i):
                            lse_part(m - 3, i, 1)
                        if there(m - 1, i):
                            queries_lo(m - 1, i)
                        if there(m - 3, i):
                            lse_part(m - 3, i, 2)
                    if k == 1 and there(m - 3, i):
                        lse_keep(m - 3, i)
                    if k in (1, 5) and there(m - 2, i):
                        small_max(m - 2, k // 4, i)
                    if k == max(Y_PRODUCTS) and there(m - Y_LAG, i):
                        add_output(m - Y_LAG, i)
                    if k == 5 and there(m - 2, i):
                        less_max(m - 2, i)
                    if k == 4 and there(m - 4, i):
                        heads_hi(m - 4, i)
                    if k in (4, 7) and there(m - 2, i):
                        small_sums(m - 2, k // 6, i)
                    if k == 4 and there(m - 4, i):
                        heads_lo(m - 4, i)
                    if m % QC == 0 and k < QC and there(m, i):
                        if k == 0:
                            if due(n_due := count(1, m, i)):
                                dve.wait_ge(q_acc, n_due)
                        split_hi(piece(m, i, k), i, xs[:, HI, k, :])

            dve.wait_ge(const_in, 48)
            in_slots(dve, slot, 2)


WEIGHTS = {"k_txt": "to_k_w", "v_txt": "to_v_w", "k_obj": "to_k_object_w", "v_obj": "to_v_object_w",
           "k_oth": "to_k_others_w", "v_oth": "to_v_others_w", "k_ip": "to_k_ip_w", "v_ip": "to_v_ip_w",
           "wq": "to_q_w", "wo": "to_out_w"}


def build(nc, d):
    project_context(nc, d)
    attend(nc, d)


def kernel(**inputs):
    import numpy as _np
    import concourse.bacc as _bacc
    from concourse import mybir as _mybir
    from concourse.bass_utils import run_bass_kernel_spmd as _run

    x, context = _np.asarray(inputs["x"]), _np.asarray(inputs["ctx_2048"])
    host = {"xT": x.transpose(0, 2, 1), "ctxT": context.transpose(0, 2, 1)}
    by_channel = context.transpose(2, 0, 1)
    at = 0
    for g, n in (("txt", N_TXT), ("obj", N_OBJ), ("oth", N_OTH), ("rest", REST)):
        host[f"ctxT_{g}"] = by_channel[:, :, at:at + n].reshape(CTX, BATCH * n)
        at += n
    for name, source in WEIGHTS.items():
        host[name] = _np.asarray(inputs[f"L0_xattn_{source}"])
    host["wq"] = host["wq"].reshape(CH, QC, HPU, HD).transpose(0, 1, 3, 2).reshape(CH, CH)
    host["bias"] = _np.asarray(inputs["L0_xattn_to_out_b"]).reshape(QC, P).T
    bounds = [0, N_TXT, N_TXT + N_OBJ, SMALL, TOK]
    rows = _np.zeros((2 * GROUPS, TOK), _np.float32)
    for g in range(GROUPS):
        rows[[g, GROUPS + g], bounds[g]:bounds[g + 1]] = 1
    host["group_rows"] = rows
    host["ident"] = _np.eye(P, dtype=_np.float32)

    nc = _bacc.Bacc("TRN2", target_bir_lowering=False, num_devices=1)
    arrays, d = {}, {}
    for name, a in host.items():
        arrays[f"in_{name}"] = _np.ascontiguousarray(a)
        d[name] = nc.dram_tensor(f"in_{name}", a.shape, F32, kind="ExternalInput").ap()
    d["kT"] = nc.dram_tensor("kT", (BATCH, 2, CH, TOK), F32, kind="Internal").ap()
    for g, n in (("txt", N_TXT), ("obj", N_OBJ), ("oth", N_OTH), ("rest", REST)):
        d[f"v_{g}_rows"] = nc.dram_tensor(f"v_{g}_rows", (BATCH * n, CH), F32, kind="Internal").ap()
    d["v_ip_rows"] = nc.dram_tensor("v_ip_rows", (BATCH, TOK - P, CH), F32, kind="Internal").ap()
    d["yT"] = nc.dram_tensor("out_yT", (BATCH, CH, TOK), F32, kind="ExternalOutput").ap()
    build(nc, d)
    r = _run(nc, [arrays], core_ids=[0])
    return _np.ascontiguousarray(r.results[0]["out_yT"].transpose(0, 2, 1))
```

```python
from contextlib import ExitStack

import concourse.bass as bass
from concourse import mybir

ALU = mybir.AluOpType
ACT = mybir.ActivationFunctionType
AX_X = mybir.AxisListType.X
F32 = mybir.dt.float32
F32R = mybir.dt.float32r
BF16 = mybir.dt.bfloat16

BATCH = 16
TOK = 512
CH = 640
CTX = 1024
HD = 32
P = 128
QC = CH // P
CC = CTX // P
HPU = P // HD
N_TXT, N_OBJ, N_OTH = 77, 4, 4
SMALL = N_TXT + N_OBJ + N_OTH
N_IP = TOK - SMALL
REST = P - SMALL
GROUPS = 4
SCALE = float(HD) ** -0.5

HI, LO = 0, 1
PASSES = ((HI, HI), (HI, LO), (LO, HI))

IPN = TOK - SMALL + 1
TXT_B = 4
REST_B = 8
N_TXT_RUNS = BATCH // TXT_B
N_REST_RUNS = BATCH // REST_B
RUN_OBJ = N_TXT_RUNS
RUN_OTH = RUN_OBJ + 1
RUN_REST = RUN_OTH + 1
RUN_IP = RUN_REST + N_REST_RUNS
RUNS = RUN_IP + BATCH
RAW = 4
WS = 3


def v_tiles(n):
    return [(a, min(P, n - a)) for a in range(0, n, P)]


def due(count):
    return not isinstance(count, int) or count > 0


def project_context(nc, d):
    with ExitStack() as ctx:
        def sb(name, shape, dt):
            return ctx.enter_context(nc.sbuf_tensor(name, shape, dt))

        def sem(name):
            return ctx.enter_context(nc.semaphore(name))

        w = sb("w_split", [P, WS, 2, CC, CH], F32R)
        c = sb("ctx_split", [P, 2, 2, CC, IPN], F32R)
        raw = sb("raw", [P, RAW, CH], F32)
        k_out = sb("k_out", [P, 2, 2, TOK], F32R)
        v_out = sb("v_out", [P, 2, CH], F32)
        k_ps = ctx.enter_context(nc.psum_tensor("k_ps", [P, 2, 512], F32))
        v_ps = ctx.enter_context(nc.psum_tensor("v_ps", [P, 2, 2, 512], F32))

        raw_in = [sem(f"raw_in{r}") for r in range(RAW)]
        piece_hi = sem("piece_hi")
        piece_lo = sem("piece_lo")
        k_acc = sem("k_acc")
        k_hi = sem("k_hi")
        k_lo = sem("k_lo")
        v_acc = sem("v_acc")
        v_sb = sem("v_sb")
        k_stored = [sem(f"k_stored{r}") for r in range(2)]
        v_stored = [sem(f"v_stored{r}") for r in range(2)]

        W_ORDER = [("k_txt", 0, None), ("v_txt", 1, None), ("k_obj", 2, (0, "v")), ("v_obj", 0, (RUN_OBJ - 1, "k")),
                   ("k_oth", 1, (RUN_OBJ - 1, "v")), ("v_oth", 2, (RUN_OBJ, "k")), ("k_ip", 0, (RUN_OBJ, "v")),
                   ("v_ip", 1, (RUN_OTH, "k"))]
        SLOT = {name: slot for name, slot, _ in W_ORDER}

        def group_of(run):
            return ("txt" if run < RUN_OBJ else "obj" if run < RUN_OTH else "oth" if run < RUN_REST else
                    "rest" if run < RUN_IP else "ip")

        def width(run):
            return {"txt": TXT_B * N_TXT, "obj": BATCH * N_OBJ, "oth": BATCH * N_OTH, "rest": REST_B * REST,
                    "ip": IPN}[group_of(run)]

        def k_blocks(run):
            return 0 if group_of(run) == "rest" else QC

        def tiles(run):
            if group_of(run) == "ip":
                return [(P * (t + 1) - SMALL + 1, P) for t in range(TOK // P - 1)]
            return v_tiles(width(run))

        k_base, v_base, lots = [0], [0], []
        for run in range(RUNS):
            k_base.append(k_base[-1] + k_blocks(run))
            v_base.append(v_base[-1] + len(tiles(run)))
        lots += [("w", "k_txt"), ("c", 0), ("w", "v_txt")]
        for run in range(RUNS - 1):
            lots += [("c", run + 1)] + [("w", name) for part in "kv" for name, _, after in W_ORDER
                                        if after == (run, part)]
        LOT = {lot: n for n, lot in enumerate(lots)}

        def piece_no(kind, which, n):
            lot = LOT[(kind, which)]
            return 2 * n + lot if lot < 2 else CC * lot + n

        def pieces_upto(kind, which):
            return piece_no(kind, which, CC - 1) + 1

        def k_needs(run):
            if group_of(run) == "rest":
                return max(pieces_upto("c", run), pieces_upto("w", "v_ip"))
            return max(pieces_upto("c", run), pieces_upto("w", f"k_{group_of(run)}"))

        def v_needs(run):
            g = group_of(run)
            return pieces_upto("w", f"v_{'ip' if g == 'rest' else g}")

        def steps(run):
            blocks, n_tiles = k_blocks(run), len(tiles(run))
            at_k = [name for name, _, after in W_ORDER if after == (run, "k")]
            at_v = [name for name, _, after in W_ORDER if after == (run, "v")]
            n_steps = max(blocks + n_tiles, CC // 2)
            for n in range(n_steps):
                yield (range(2 * n, 2 * n + 2) if run < RUNS - 1 and n < CC // 2 else (),
                       n if n < blocks else None, n - blocks if blocks <= n < blocks + n_tiles else None,
                       at_k if n == blocks else [], at_v if n == n_steps - 1 else [])

        PER_TURN = 2
        TURNS = (BATCH - PER_TURN) // PER_TURN
        D_PIECE, D_K, D_V = PER_TURN * CC, PER_TURN * QC, PER_TURN * len(tiles(RUN_IP))

        def ctx_src(run0, i, n):
            g, rows = group_of(run0), slice(n * P, (n + 1) * P)
            if g == "ip":
                return d["ctxT"][run0 - RUN_IP + PER_TURN * i, rows, TOK - IPN:TOK]
            if g == "txt":
                return d["ctxT_txt"][rows, run0 * width(0):(run0 + 1) * width(0)]
            if g == "rest":
                return d["ctxT_rest"][rows, (run0 - RUN_REST) * width(run0):(run0 - RUN_REST + 1) * width(run0)]
            return d[f"ctxT_{g}"][rows, :]

        def in_turns(eng, one_run):
            for run in range(RUN_IP):
                one_run(run, 0)
            with eng.Fori(0, TURNS) as i:
                for run in range(RUN_IP, RUN_IP + PER_TURN):
                    one_run(run, i)
            for run in range(RUNS - PER_TURN, RUNS):
                one_run(run, 0)

        block = ctx.enter_context(nc.Block())

        @block.sync
        def _(sp):
            def load(k0, i, src):
                if due(n_due := k0 - RAW + 1 + D_PIECE * i):
                    sp.wait_ge(piece_lo, n_due)
                sp.dma_start(raw[:, k0 % RAW, 0:src.shape[-1]], src).then_inc(raw_in[k0 % RAW], 16)

            def load_w(name, n):
                load(piece_no("w", name, n), 0, d[name][n * P:(n + 1) * P, :])

            for n in range(CC):
                load_w("k_txt", n)
                load(piece_no("c", 0, n), 0, ctx_src(0, 0, n))
            for n in range(CC):
                load_w("v_txt", n)

            def store_k(run0, i, m):
                k0, g, n = k_base[run0] + m, group_of(run0), width(run0)
                sp.wait_ge(k_lo, k0 + 1 + D_K * i)
                for part in (HI, LO):
                    rows = slice(m * P, (m + 1) * P)
                    if g == "ip":
                        dst = d["kT"][run0 - RUN_IP + PER_TURN * i, part, rows, SMALL:TOK]
                        src = k_out[:, k0 % 2, part, 1:n]
                    else:
                        at, size = {"txt": (0, N_TXT), "obj": (N_TXT, N_OBJ), "oth": (N_TXT + N_OBJ, N_OTH)}[g]
                        b0 = TXT_B * run0 if g == "txt" else 0
                        dst = d["kT"][b0:b0 + n // size, part, rows, at:at + size].rearrange("b p t -> p b t")
                        src = k_out[:, k0 % 2, part, 0:n].rearrange("p (b t) -> p b t", t=size)
                    sp.dma_start(dst, src.bitcast(F32)).then_inc(k_stored[k0 % 2], 16)

            def store_v(run0, i, t):
                v0, g, (a, rows) = v_base[run0] + t, group_of(run0), tiles(run0)[t]
                if g == "ip":
                    dst = d["v_ip_rows"][run0 - RUN_IP + PER_TURN * i, t * P:(t + 1) * P, :]
                else:
                    a += {"txt": run0, "rest": run0 - RUN_REST}.get(g, 0) * width(run0)
                    dst = d[f"v_{g}_rows"][a:a + rows, :]
                sp.wait_ge(v_sb, v0 + 1 + D_V * i)
                sp.dma_start(dst, v_out[0:rows, v0 % 2, :]).then_inc(v_stored[v0 % 2], 16)

            def one_run(run0, i):
                def store(step):
                    if step and step[1] is not None:
                        store_k(run0, i, step[1])
                    if step and step[2] is not None:
                        store_v(run0, i, step[2])

                before = None
                for step in steps(run0):
                    pieces, _, _, at_k, at_v = step
                    for n in pieces:
                        load(piece_no("c", run0 + 1, n), i, ctx_src(run0 + 1, i, n))
                    for name in at_k:
                        for n in range(CC):
                            load_w(name, n)
                    store(before)
                    for name in at_v:
                        for n in range(CC):
                            load_w(name, n)
                    before = step
                store(before)

            in_turns(sp, one_run)
            for r in range(2):
                sp.wait_ge(k_stored[r], 32 * ((k_base[RUNS] - r + 1) // 2))
                sp.wait_ge(v_stored[r], 16 * ((v_base[RUNS] - r + 1) // 2))

        @block.scalar
        def _(act):
            def split_hi(k0, i, dst, n):
                act.wait_ge(raw_in[k0 % RAW], 16 * (k0 // RAW + 1) + 16 * (D_PIECE // RAW) * i)
                nc.scalar.activation(dst, raw[:, k0 % RAW, 0:n], ACT.Copy).then_inc(piece_hi, 1)

            def split_ctx(run0, i, n):
                if n == 0:
                    if due(n_due := v_base[max(run0 - 1, 0)] + D_V * i):
                        act.wait_ge(v_acc, n_due)
                split_hi(piece_no("c", run0, n), i, c[:, run0 % 2, HI, n, 0:width(run0)], width(run0))

            def split_w(name, n, after=None):
                if n == 0 and after:
                    if after[1] == "k":
                        act.wait_ge(k_acc, k_base[after[0] + 1])
                    else:
                        act.wait_ge(v_acc, v_base[after[0] + 1])
                split_hi(piece_no("w", name, n), 0, w[:, SLOT[name], HI, n, :], CH)

            for n in range(CC):
                split_w("k_txt", n)
                split_ctx(0, 0, n)
            for n in range(CC):
                split_w("v_txt", n)

            def keep_k(run0, i, m):
                k0, n = k_base[run0] + m, width(run0)
                act.wait_ge(k_acc, k0 + 1 + D_K * i)
                if due(n_due := 32 * (k0 // 2) + 16 * D_K * i):
                    act.wait_ge(k_stored[k0 % 2], n_due)
                nc.scalar.activation(k_out[:, k0 % 2, HI, 0:n], k_ps[:, k0 % 2, 0:n], ACT.Copy).then_inc(k_hi, 1)

            def keep_v(run0, i, t):
                v0, rows = v_base[run0] + t, tiles(run0)[t][1]
                act.wait_ge(v_acc, v0 + 1 + D_V * i)
                if due(n_due := 16 * (v0 // 2) + 8 * D_V * i):
                    act.wait_ge(v_stored[v0 % 2], n_due)
                nc.scalar.activation(v_out[0:rows, v0 % 2, :].rearrange("p (a n) -> p a n", a=2),
                                     v_ps[0:rows, v0 % 2, :, 0:CH // 2], ACT.Copy).then_inc(v_sb, 1)

            def one_run(run0, i):
                for pieces, block_m, tile, at_k, at_v in steps(run0):
                    for n in pieces:
                        split_ctx(run0 + 1, i, n)
                    for name in at_k:
                        for n in range(CC):
                            split_w(name, n, (run0, "k"))
                    if block_m is not None:
                        keep_k(run0, i, block_m)
                    if tile is not None:
                        keep_v(run0, i, tile)
                    for name in at_v:
                        for n in range(CC):
                            split_w(name, n, (run0, "v"))

            in_turns(act, one_run)

        @block.vector
        def _(dve):
            def split_lo(k0, i, hi, lo, n):
                dve.wait_ge(piece_hi, k0 + 1 + D_PIECE * i)
                nc.vector.tensor_tensor(lo, raw[:, k0 % RAW, 0:n], hi.bitcast(F32), ALU.subtract).then_inc(piece_lo, 1)

            def split_ctx(run0, i, n):
                b, wd = run0 % 2, width(run0)
                split_lo(piece_no("c", run0, n), i, c[:, b, HI, n, 0:wd], c[:, b, LO, n, 0:wd], wd)

            def split_w(name, n):
                s = SLOT[name]
                split_lo(piece_no("w", name, n), 0, w[:, s, HI, n, :], w[:, s, LO, n, :], CH)

            for n in range(CC):
                split_w("k_txt", n)
                split_ctx(0, 0, n)
            for n in range(CC):
                split_w("v_txt", n)

            def keep_k(run0, i, m):
                k0, n = k_base[run0] + m, width(run0)
                dve.wait_ge(k_hi, k0 + 1 + D_K * i)
                nc.vector.tensor_tensor(k_out[:, k0 % 2, LO, 0:n], k_ps[:, k0 % 2, 0:n],
                                        k_out[:, k0 % 2, HI, 0:n].bitcast(F32), ALU.subtract).then_inc(k_lo, 1)

            def one_run(run0, i):
                for pieces, block_m, _, at_k, at_v in steps(run0):
                    for n in pieces:
                        split_ctx(run0 + 1, i, n)
                    for name in at_k:
                        for n in range(CC):
                            split_w(name, n)
                    if block_m is not None:
                        keep_k(run0, i, block_m)
                    for name in at_v:
                        for n in range(CC):
                            split_w(name, n)

            in_turns(dve, one_run)

        @block.tensor
        def _(pe):
            def one_run(run0, i):
                g, n, b = group_of(run0), width(run0), run0 % 2
                wg = "ip" if g == "rest" else g
                if run0 > 0:
                    pe.wait_ge(piece_lo, k_needs(run0) + D_PIECE * i)
                for m in range(k_blocks(run0)):
                    k0, s = k_base[run0] + m, SLOT[f"k_{wg}"]
                    if due(n_due := k0 - 1 + D_K * i):
                        pe.wait_ge(k_lo, n_due)
                    for q in range(CC):
                        if k0 == 0:
                            pe.wait_ge(piece_lo, piece_no("c", 0, q) + 1)
                        for z, (pw, px) in enumerate(PASSES):
                            last = nc.tensor.matmul(k_ps[:, k0 % 2, 0:n], w[:, s, pw, q, m * P:(m + 1) * P],
                                                    c[:, b, px, q, 0:n], start=(q == 0 and z == 0),
                                                    stop=(q == CC - 1 and z == len(PASSES) - 1))
                    last.then_inc(k_acc, 1)
                s = SLOT[f"v_{wg}"]
                if v_needs(run0) > k_needs(run0):
                    pe.wait_ge(piece_lo, v_needs(run0))
                for t, (a, rows) in enumerate(tiles(run0)):
                    v0 = v_base[run0] + t
                    if due(n_due := v0 - 1 + D_V * i):
                        pe.wait_ge(v_sb, n_due)
                    for half in range(2):
                        for q in range(CC):
                            for z, (px, pw) in enumerate(PASSES):
                                last = nc.tensor.matmul(
                                    v_ps[0:rows, v0 % 2, half, 0:CH // 2], c[:, b, px, q, a:a + rows],
                                    w[:, s, pw, q, half * (CH // 2):(half + 1) * (CH // 2)],
                                    start=(q == 0 and z == 0), stop=(q == CC - 1 and z == len(PASSES) - 1))
                    last.then_inc(v_acc, 1)

            in_turns(pe, one_run)


UNITS = BATCH * QC
RING = 3
LOOP = RING * QC
STEPS = 8
QT = TOK // P
KT = TOK // P
PAIRS = HPU * QT // 2
ITEMS = HPU * KT
PR = 6
XR = 5
HR = 2 * QC
W_COLS = CH // 2
ROWS_S = 3 * HD
ROWS_ST = ROWS_S + 2 * GROUPS
BLOCKS = ((HI, HI), (LO, HI), (HI, LO))
IP = GROUPS - 1
PARTS = ((0, HPU // 2), (HPU // 2, HPU))
PAIRS_UPTO = [2 * to for _, to in PARTS]
Q_PRODUCTS = {6: (0, 4), 7: (4, 10)}
Y_LAG = 9
Y_PRODUCTS = {2: (0, 4), 3: (4, 8), 4: (8, 12), 5: (12, 15)}


def attend(nc, d):
    with ExitStack() as ctx:
        def sb(name, shape, dt):
            return ctx.enter_context(nc.sbuf_tensor(name, shape, dt))

        def psum(name, shape):
            return ctx.enter_context(nc.psum_tensor(name, shape, F32))

        def sem(name):
            return ctx.enter_context(nc.semaphore(name))

        wq = sb("wq", [P, 2, QC, CH], F32R)
        wo = sb("wo", [P, 2, QC, CH], F32R)
        xraw = sb("xraw", [P, XR, TOK], F32)
        xs = sb("xs", [P, 2, QC, TOK], F32R)
        q_out = sb("q_out", [P, 2, TOK], F32R)
        qpack = sb("qpack", [P, RING, HPU, TOK], F32R)
        kpack = sb("kpack", [P, RING, HPU, TOK], F32R)
        vt = sb("vt", [P, RING, KT, P], F32)
        small = sb("small", [P, HPU * QT, SMALL], F32)
        negmax = sb("negmax", [P, RING, GROUPS, HPU, QT], F32)
        sums = sb("sums", [P, RING, GROUPS, HPU, QT], F32)
        logs = sb("logs", [P, GROUPS, HPU, QT], F32)
        neglse = sb("neglse", [P, GROUPS, HPU, QT], F32)
        neglse2 = sb("neglse2", [P, 2, GROUPS, HPU, QT], F32R)
        lse_rows = sb("lse_rows", [2 * GROUPS * HPU, TOK], F32R)
        probs = sb("probs", [P, PR, TOK], F32)
        heads = sb("heads", [P, HR, 2, TOK], F32R)
        out = sb("out", [P, RING, TOK], F32)
        ident = sb("ident", [P, P], F32)
        bias = sb("bias", [P, QC], F32)

        s_ps = psum("s_ps", [P, 2, 2, 512])
        st_ps = psum("st_ps", [P, 2, 512])
        o_ps = psum("o_ps", [P, 512])
        m_ps = psum("m_ps", [P, 512])

        const_in = sem("const_in")
        raw_in = [sem(f"raw2_in{r}") for r in range(XR)]
        x_hi, x_lo = sem("x_hi"), sem("x_lo")
        rows_set = sem("rows_set")
        q_acc, q_hi, q_lo = sem("q_acc"), sem("q_hi"), sem("q_lo")
        q_packed = [sem(f"q_packed{r}") for r in range(RING)]
        k_packed = [sem(f"k_packed{r}") for r in range(RING)]
        v_in = [sem(f"v_in{r}") for r in range(RING)]
        s_done = sem("s_done")
        s_max = sem("s_max")
        s_exp = sem("s_exp")
        row_max = sem("row_max")
        sm_sub = sem("sm_sub")
        sm_exp = sem("sm_exp")
        sm_sum = sem("sm_sum")
        ln_done = sem("ln_done")
        lse_step = sem("lse_step")
        lse_t = sem("lse_t")
        lse_sb = sem("lse_sb")
        lse_packed = [sem(f"lse_packed{r}") for r in range(RING)]
        st_done = sem("st_done")
        p_done = sem("p_done")
        pv_done = sem("pv_done")
        o_hi, o_lo = sem("o_hi"), sem("o_lo")
        y_done = sem("y_done")
        y_added = sem("y_added")
        res_in = [sem(f"res_in{r}") for r in range(RING)]
        y_out = [sem(f"y_out{r}") for r in range(RING)]

        def count(per, k, i, more=0):
            return per * k + more + per * LOOP * i

        def use(k, i):
            return k // RING + 1 + (LOOP // RING) * i

        def batch(k, i):
            return k // QC + (LOOP // QC) * i

        def there(k, i):
            return 0 <= k < UNITS if isinstance(i, int) else True

        PRELUDE = 20
        TURNS = (UNITS - PRELUDE) // LOOP
        assert PRELUDE >= Y_LAG and PRELUDE + TURNS * LOOP == UNITS and TURNS % 2 == 0
        assert LOOP % RING == 0 and LOOP * ITEMS % PR == 0 and LOOP % XR == 0 and 2 * LOOP % HR == 0

        def in_slots(eng, slot, at_once=1):
            for m in range(PRELUDE):
                slot(m, 0)
            with eng.Fori(0, TURNS, at_once) as i:
                for m in range(PRELUDE, PRELUDE + at_once * LOOP):
                    slot(m, i)
            for m in range(UNITS, UNITS + Y_LAG):
                slot(m, 0)

        def pair_at(m, k):
            return (m - 1, k - 6) if k >= 6 else (m - 2, k + 2)

        def items_at(m, k):
            u, at = (m - 3, k - 3) if k >= 3 else (m - 4, k + 5)
            return u, (2 * at, 2 * at + 1)

        def small_groups(h):
            s = small[:, QT * PARTS[h][0]:QT * PARTS[h][1], :]
            return s[:, :, 0:N_TXT], s[:, :, N_TXT:SMALL].rearrange("p w (g n) -> p w g n", g=2)

        def small_stats(tile, u, h):
            s = tile[:, u % RING, :, PARTS[h][0]:PARTS[h][1], :].rearrange("p g j t -> p (j t) g")
            return s[:, :, 0], s[:, :, 1:IP]

        def over_keys(stats, n):
            dims = len(stats.shape)
            return stats.unsqueeze(dims).to_broadcast([*stats.shape, n])

        small_rows = small[ROWS_S:ROWS_ST, :, :].rearrange("p w n -> p (w n)")[:, 0:TOK]

        def weight_pieces(first):
            for c in range(QC):
                for n, at in enumerate(range(0, CH, W_COLS)):
                    yield first + c * (CH // W_COLS) + n, c, slice(at, at + W_COLS)

        PIECES_WQ = QC * (CH // W_COLS)
        PIECES_W = 2 * PIECES_WQ

        def piece(k, i, c):
            return (PIECES_WQ if isinstance(i, int) and k == 0 else PIECES_W) + k + c

        WO_FIRST = PIECES_WQ + QC

        block = ctx.enter_context(nc.Block())

        @block.sync
        def _(sp):
            sp.dma_start(ident[:, :], d["ident"]).then_inc(const_in, 16)
            sp.dma_start(bias[:, :], d["bias"]).then_inc(const_in, 16)
            sp.dma_start(small_rows, d["group_rows"]).then_inc(const_in, 16)

            def load(n, i, src):
                if due(n_due := n - XR + 1 + LOOP * i):
                    sp.wait_ge(x_lo, n_due)
                sp.dma_start(xraw[:, n % XR, 0:src.shape[-1]], src).then_inc(raw_in[n % XR], 16)

            for n, c, cols in weight_pieces(0):
                load(n, 0, d["wq"][c * P:(c + 1) * P, cols])

            def pack_keys(u, i):
                r, b, cols = u % RING, batch(u, i), slice(u % QC * P, (u % QC + 1) * P)
                if due(n_due := count(ITEMS, u - RING + 1, i)):
                    sp.wait_ge(st_done, n_due)
                for n, (_, part) in enumerate(BLOCKS):
                    sp.dma_start(kpack[n * HD:(n + 1) * HD, r, :, :].bitcast(F32),
                                 d["kT"][b, part, cols, :].rearrange("(j c) t -> c j t", c=HD)).then_inc(k_packed[r], 16)

            def pack_queries(u, i):
                r = u % RING
                sp.wait_ge(q_lo, count(1, u, i, 1))
                for n, (part, _) in enumerate(BLOCKS):
                    sp.dma_start(qpack[n * HD:(n + 1) * HD, r, :, :].bitcast(F32), q_out[:, part, :].bitcast(F32)).then_inc(q_packed[r], 16)

            def load_values(u, i):
                r, b, cols = u % RING, batch(u, i), slice(u % QC * P, (u % QC + 1) * P)
                if due(n_due := count(KT, u - RING + 1, i)):
                    sp.wait_ge(pv_done, n_due)
                row = 0
                for g, n in (("txt", N_TXT), ("obj", N_OBJ), ("oth", N_OTH), ("rest", REST)):
                    sp.dma_start(vt[row:row + n, r, 0, :], d[f"v_{g}_rows"][bass.ds(b * n, n), cols]).then_inc(v_in[r], 16)
                    row += n
                sp.dma_start(vt[:, r, 1:KT, :], d["v_ip_rows"][b, :, cols].rearrange("(t p) n -> p t n", p=P))\
                    .then_inc(v_in[r], 16)

            def rows_of(w, i):
                return batch(w, i), slice(w % QC * P, (w % QC + 1) * P)

            def slot(m, i):
                if m % QC == 0 and there(m, i):
                    for c in range(QC):
                        load(piece(m, i, c), i, d["xT"][batch(m, i), c * P:(c + 1) * P, :])
                if m == 2:
                    for n, c, cols in weight_pieces(WO_FIRST):
                        load(n, 0, d["wo"][c * P:(c + 1) * P, cols])
                w = m - Y_LAG - 1
                if there(w, i):
                    b, rows = rows_of(w, i)
                    sp.wait_ge(y_added, count(1, w, i, 1))
                    sp.dma_start(d["yT"][b, rows, :], out[:, w % RING, :]).then_inc(y_out[w % RING], 16)
                w = m - Y_LAG
                if there(w, i):
                    b, rows = rows_of(w, i)
                    if due(n_due := 16 * (use(w, i) - 1)):
                        sp.wait_ge(y_out[w % RING], n_due)
                    sp.dma_start(out[:, w % RING, :], d["xT"][b, rows, :]).then_inc(res_in[w % RING], 16)
                if there(m - 2, i):
                    load_values(m - 2, i)
                u = m - 3
                if there(u, i):
                    sp.wait_ge(lse_sb, count(1, u, i, 1))
                    sp.dma_start(qpack[ROWS_S:ROWS_ST, u % RING, :, :].bitcast(F32), lse_rows[:, :].bitcast(F32)).then_inc(lse_packed[u % RING], 16)
                if there(m - 1, i):
                    pack_keys(m - 1, i)
                    pack_queries(m - 1, i)

            in_slots(sp, slot)
            w = UNITS - 1
            b, rows = rows_of(w, 0)
            sp.wait_ge(y_added, UNITS)
            sp.dma_start(d["yT"][b, rows, :], out[:, w % RING, :]).then_inc(y_out[w % RING], 16)
            for r in range(RING):
                sp.wait_ge(y_out[r], 16 * len(range(r, UNITS, RING)))

        @block.gpsimd
        def _(pool):
            def split_lo(n, i, hi, lo):
                pool.wait_ge(x_hi, n + 1 + LOOP * i)
                nc.gpsimd.tensor_tensor(lo, xraw[:, n % XR, 0:TOK], hi.bitcast(F32), ALU.subtract).then_inc(x_lo, 1)

            def less_max(u, i):
                txt, two = small_groups(0)
                m_txt, m_two = small_stats(negmax, u, 0)
                pool.wait_ge(row_max, count(4, u, i, 2))
                nc.gpsimd.tensor_tensor(txt, txt, over_keys(m_txt, N_TXT), ALU.add).then_inc(sm_sub, 1)
                nc.gpsimd.tensor_tensor(two, two, over_keys(m_two, N_OBJ), ALU.add).then_inc(sm_sub, 1)

            def slot(m, i):
                if m == 0:
                    pool.wait_ge(x_lo, PIECES_WQ)
                if m == QC:
                    pool.wait_ge(x_lo, PIECES_W + QC)
                for k in range(STEPS):
                    if m % QC == 0 and k < QC and there(m, i):
                        split_lo(piece(m, i, k), i, xs[:, HI, k, :], xs[:, LO, k, :])
                    if k == 2 and there(m - 2, i):
                        less_max(m - 2, i)

            in_slots(pool, slot)

        @block.tensor
        def _(pe):
            pe.wait_ge(const_in, 48)
            pe.wait_ge(rows_set, RING)

            def scores(u, p, i):
                j, t0, n = p // 2, 2 * (p % 2), PAIRS * u + p
                if p == 0:
                    pe.wait_ge(q_packed[u % RING], 16 * len(BLOCKS) * use(u, i))
                    pe.wait_ge(k_packed[u % RING], 16 * len(BLOCKS) * use(u, i))
                if due(n_due := count(PAIRS, u, i, p - 1)):
                    pe.wait_ge(s_exp, n_due)
                for z in range(2):
                    t = t0 + z
                    last = nc.tensor.matmul(s_ps[:, n % 2, z, :], qpack[0:ROWS_S, u % RING, j, t * P:(t + 1) * P],
                                            kpack[0:ROWS_S, u % RING, j, :], start=True, stop=True)
                last.then_inc(s_done, 1)

            def scores_t(u, items, i):
                r = u % RING
                if items[0] == 0:
                    pe.wait_ge(lse_packed[r], 16 * use(u, i))
                for x in items:
                    kt, j = x // HPU, x % HPU
                    if due(n_due := count(ITEMS, u, i, x - 1)):
                        pe.wait_ge(p_done, n_due)
                    nc.tensor.matmul(st_ps[:, x % 2, :], kpack[0:ROWS_ST, r, j, kt * P:(kt + 1) * P],
                                     qpack[0:ROWS_ST, r, j, :], start=True, stop=True).then_inc(st_done, 1)

            def values(u, kt, i):
                r = u % RING
                if kt == 0:
                    pe.wait_ge(v_in[r], 16 * 5 * use(u, i))
                    if due(n_due := count(1, u, i)):
                        pe.wait_ge(o_lo, n_due)
                pe.wait_ge(p_done, count(ITEMS, u, i, HPU * (kt + 1)))
                for j in range(HPU):
                    last = nc.tensor.matmul(o_ps[j * HD:(j + 1) * HD, :], vt[:, r, kt, j * HD:(j + 1) * HD],
                                            probs[:, (ITEMS * u + HPU * kt + j) % PR, :], start=(kt == 0), stop=(kt == KT - 1))
                last.then_inc(pv_done, 1)

            def queries(u, i, products):
                if products[0] == 0:
                    if there(u - Y_LAG, i):
                        pe.wait_ge(y_added, count(1, u - Y_LAG, i, 1))
                    else:
                        if due(n_due := count(1, u - 2, i)):
                            pe.wait_ge(lse_sb, n_due)
                    pe.wait_ge(x_lo, piece(u // QC * QC, i, QC) + LOOP * i)
                cols = slice(u % QC * P, (u % QC + 1) * P)
                for n in products:
                    c, (pw, px) = n // len(PASSES), PASSES[n % len(PASSES)]
                    last = nc.tensor.matmul(m_ps[:, :], wq[:, pw, c, cols], xs[:, px, c, :], start=(n == 0),
                                            stop=(n == QC * len(PASSES) - 1))
                if products[-1] == QC * len(PASSES) - 1:
                    last.then_inc(q_acc, 1)

            def transpose_lse(u, i):
                pe.wait_ge(q_lo, count(1, u, i, 3) if there(u + 2, i) else UNITS)
                if not there(u + 2, i):
                    pe.wait_ge(y_added, count(1, u + 3 - Y_LAG, i))
                pe.wait_ge(lse_step, count(3, u, i, 3))
                for t in range(QT):
                    last = nc.tensor.transpose(m_ps[0:2 * GROUPS * HPU, t * P:(t + 1) * P],
                                               neglse2[:, :, :, :, t].bitcast(F32).rearrange("p a g j -> p (a g j)"),
                                               ident[:, :])
                last.then_inc(lse_t, 1)

            def output(w, i, products):
                if products[0] == 0:
                    if w == 0:
                        pe.wait_ge(x_lo, PIECES_W + QC)
                    pe.wait_ge(o_lo, count(1, w // QC * QC, i, QC))
                    if there(w + Y_LAG - 3, i):
                        pe.wait_ge(lse_sb, count(1, w + Y_LAG - 3, i, 1))
                    else:
                        pe.wait_ge(y_added, count(1, w, i))
                cols = slice(w % QC * P, (w % QC + 1) * P)
                for n in products:
                    z, (pw, po) = n // len(PASSES), PASSES[n % len(PASSES)]
                    last = nc.tensor.matmul(m_ps[:, :], wo[:, pw, z, cols], heads[:, (w // QC * QC + z) % HR, po, :],
                                            start=(n == 0), stop=(n == QC * len(PASSES) - 1))
                if products[-1] == QC * len(PASSES) - 1:
                    last.then_inc(y_done, 1)

            def slot(m, i):
                for k in range(STEPS):
                    u, p = pair_at(m, k)
                    if there(u, i):
                        scores(u, p, i)
                    u, items = items_at(m, k)
                    if there(u, i):
                        scores_t(u, items, i)
                    if k == 0 and there(m - 1, i):
                        queries(m - 1, i, range(Q_PRODUCTS[STEPS - 1][1], QC * len(PASSES)))
                    if k == 1 and there(m - 3, i):
                        transpose_lse(m - 3, i)
                    if k in Y_PRODUCTS and there(m - Y_LAG, i):
                        output(m - Y_LAG, i, range(*Y_PRODUCTS[k]))
                    if k in Q_PRODUCTS and there(m, i):
                        queries(m, i, range(*Q_PRODUCTS[k]))
                    for at, lag, kt in ((5, 3, 0), (7, 3, 1), (1, 4, 2), (3, 4, 3)):
                        if k == at and there(m - lag, i):
                            values(m - lag, kt, i)

            in_slots(pe, slot, 2)

        @block.scalar
        def _(act):
            def split_hi(n, i, dst, width):
                act.wait_ge(raw_in[n % XR], 16 * (n // XR + 1) + 16 * (LOOP // XR) * i)
                nc.scalar.activation(dst, xraw[:, n % XR, 0:width], ACT.Copy).then_inc(x_hi, 1)

            nc.scalar.preload_act_table_set("natural_log_exp_and_others")
            for n, c, cols in weight_pieces(0):
                split_hi(n, 0, wq[:, HI, c, cols], W_COLS)

            def prob(u, items, i):
                for x in items:
                    act.wait_ge(st_done, count(ITEMS, u, i, x + 1))
                    if x % 2 == 0:
                        if due(n_due := count(KT, u, i, (x + 1 - PR) // HPU + 1)):
                            act.wait_ge(pv_done, n_due)
                    nc.scalar.activation(probs[:, (ITEMS * u + x) % PR, :], st_ps[:, x % 2, :], ACT.Exp).then_inc(p_done, 1)

            def ip_sums(u, p, i):
                j, t0, n, r = p // 2, 2 * (p % 2), PAIRS * u + p, u % RING
                act.wait_ge(s_max, count(2 * PAIRS, u, i, 2 * (p + 1)))
                for z in range(2):
                    t = t0 + z
                    last = nc.scalar.activation(s_ps[:, n % 2, z, SMALL:TOK], s_ps[:, n % 2, z, SMALL:TOK], ACT.Exp,
                                                bias=negmax[:, r, IP, j, t:t + 1],
                                                accum_out=sums[:, r, IP, j, t:t + 1])
                last.then_inc(s_exp, 1)

            def small_exp(u, h, i):
                act.wait_ge(sm_sub, count(4, u, i, 2 * (h + 1)))
                part = small[:, QT * PARTS[h][0]:QT * PARTS[h][1], :]
                nc.scalar.activation(part, part, ACT.Exp).then_inc(sm_exp, 1)

            def logs_of(u, i):
                act.wait_ge(sm_sum, count(4, u, i, 4))
                act.wait_ge(s_exp, count(PAIRS, u, i, PAIRS))
                if due(n_due := count(3, u, i)):
                    act.wait_ge(lse_step, n_due)
                nc.scalar.activation(logs[:, :, :, :], sums[:, u % RING, :, :, :], ACT.Ln).then_inc(ln_done, 1)

            def slot(m, i):
                if m == 2:
                    act.wait_ge(x_hi, WO_FIRST)
                    for n, c, cols in weight_pieces(WO_FIRST):
                        split_hi(n, 0, wo[:, HI, c, cols], W_COLS)
                for k in range(STEPS):
                    u, items = items_at(m, k)
                    if there(u, i):
                        prob(u, items, i)
                    if k == 0 and there(m - 3, i):
                        logs_of(m - 3, i)
                    if k == 6 and there(m - 2, i):
                        small_exp(m - 2, 1, i)
                    u, p = pair_at(m, k)
                    if there(u, i):
                        ip_sums(u, p, i)
                    if k == 3 and there(m - 2, i):
                        small_exp(m - 2, 0, i)

            in_slots(act, slot)

        @block.vector
        def _(dve):
            def split_lo(n, i, hi, lo, width):
                dve.wait_ge(x_hi, n + 1 + LOOP * i)
                nc.vector.tensor_tensor(lo, xraw[:, n % XR, 0:width], hi.bitcast(F32), ALU.subtract).then_inc(x_lo, 1)

            dve.wait_ge(const_in, 48)
            for r in range(RING):
                nc.vector.tensor_copy(kpack[ROWS_S:ROWS_ST, r, :, :],
                                      small_rows.unsqueeze(1).to_broadcast([2 * GROUPS, HPU, TOK])).then_inc(rows_set, 1)
            for n, c, cols in weight_pieces(0):
                split_lo(n, 0, wq[:, HI, c, cols], wq[:, LO, c, cols], W_COLS)

            def pair_max(u, p, i):
                j, t0, n, r = p // 2, 2 * (p % 2), PAIRS * u + p, u % RING
                dve.wait_ge(s_done, count(PAIRS, u, i, p + 1))
                nc.vector.tensor_reduce(negmax[:, r, IP, j, t0:t0 + 2], s_ps[:, n % 2, :, SMALL:TOK], AX_X, ALU.max,
                                        negate=True).then_inc(s_max, 1)
                for h, (first, _) in enumerate(PARTS):
                    if p == 2 * first:
                        if due(n_due := count(4, u - 1, i, 2 + 2 * h)):
                            dve.wait_ge(sm_sum, n_due)
                w = j * QT + t0
                nc.vector.tensor_copy(small[:, w:w + 2, :], s_ps[:, n % 2, :, 0:SMALL]).then_inc(s_max, 1)

            def small_max(u, h, i):
                txt, two = small_groups(h)
                m_txt, m_two = small_stats(negmax, u, h)
                dve.wait_ge(s_max, count(2 * PAIRS, u, i, 2 * PAIRS_UPTO[h]))
                nc.vector.tensor_reduce(m_txt, txt, AX_X, ALU.max, negate=True).then_inc(row_max, 1)
                nc.vector.tensor_reduce(m_two, two, AX_X, ALU.max, negate=True).then_inc(row_max, 1)

            def less_max(u, i):
                txt, two = small_groups(1)
                m_txt, m_two = small_stats(negmax, u, 1)
                dve.wait_ge(row_max, count(4, u, i, 4))
                nc.vector.tensor_tensor(txt, txt, over_keys(m_txt, N_TXT), ALU.add).then_inc(sm_sub, 1)
                nc.vector.tensor_tensor(two, two, over_keys(m_two, N_OBJ), ALU.add).then_inc(sm_sub, 1)

            def small_sums(u, h, i):
                txt, two = small_groups(h)
                s_txt, s_two = small_stats(sums, u, h)
                dve.wait_ge(sm_exp, count(2, u, i, h + 1))
                nc.vector.tensor_reduce(s_txt, txt, AX_X, ALU.add).then_inc(sm_sum, 1)
                nc.vector.tensor_reduce(s_two, two, AX_X, ALU.add).then_inc(sm_sum, 1)

            def lse_part(u, i, part):
                if part == 0:
                    if due(n_due := count(1, u, i)):
                        dve.wait_ge(lse_t, n_due)
                    dve.wait_ge(ln_done, count(1, u, i, 1))
                    nc.vector.tensor_tensor(neglse[:, :, :, :], negmax[:, u % RING, :, :, :], logs[:, :, :, :],
                                            ALU.subtract).then_inc(lse_step, 1)
                else:
                    dve.wait_ge(lse_step, count(3, u, i, part))
                if part == 1:
                    nc.vector.tensor_copy(neglse2[:, HI, :, :, :], neglse[:, :, :, :]).then_inc(lse_step, 1)
                elif part == 2:
                    nc.vector.tensor_tensor(neglse2[:, LO, :, :, :], neglse[:, :, :, :],
                                            neglse2[:, HI, :, :, :].bitcast(F32), ALU.subtract).then_inc(lse_step, 1)

            def queries_hi(u, i):
                dve.wait_ge(q_acc, count(1, u, i, 1))
                if not isinstance(i, int) or u > 0:
                    dve.wait_ge(q_packed[(u - 1) % RING], 16 * len(BLOCKS) * use(u - 1, i))
                nc.vector.tensor_scalar(q_out[:, HI, :], m_ps[:, :], SCALE, None, ALU.mult).then_inc(q_hi, 1)

            def queries_lo(u, i):
                dve.wait_ge(q_hi, count(1, u, i, 1))
                nc.vector.scalar_tensor_tensor(out=q_out[:, LO, :], in0=m_ps[:, :], scalar=SCALE,
                                               in1=q_out[:, HI, :].bitcast(F32), op0=ALU.mult,
                                               op1=ALU.subtract).then_inc(q_lo, 1)

            def heads_hi(u, i):
                dve.wait_ge(pv_done, count(KT, u, i, KT))
                if due(n_due := count(1, u // QC * QC, i, -QC)):
                    dve.wait_ge(y_done, n_due)
                nc.vector.tensor_copy(heads[:, u % HR, HI, :], o_ps[:, :]).then_inc(o_hi, 1)

            def heads_lo(u, i):
                dve.wait_ge(o_hi, count(1, u, i, 1))
                nc.vector.tensor_tensor(heads[:, u % HR, LO, :], o_ps[:, :], heads[:, u % HR, HI, :].bitcast(F32),
                                        ALU.subtract).then_inc(o_lo, 1)

            def split_hi(n, i, dst):
                dve.wait_ge(raw_in[n % XR], 16 * (n // XR + 1) + 16 * (LOOP // XR) * i)
                nc.vector.tensor_copy(dst, xraw[:, n % XR, :]).then_inc(x_hi, 1)

            def lse_keep(u, i):
                dve.wait_ge(lse_t, count(1, u, i, 1))
                if not isinstance(i, int) or u > 0:
                    dve.wait_ge(lse_packed[(u - 1) % RING], 16 * use(u - 1, i))
                nc.vector.tensor_copy(lse_rows[:, :], m_ps[0:2 * GROUPS * HPU, :]).then_inc(lse_sb, 1)

            def add_output(w, i):
                dve.wait_ge(y_done, count(1, w, i, 1))
                dve.wait_ge(res_in[w % RING], 16 * use(w, i))
                nc.vector.scalar_tensor_tensor(out=out[:, w % RING, :], in0=m_ps[:, :],
                                               scalar=bias[:, w % QC:w % QC + 1], in1=out[:, w % RING, :],
                                               op0=ALU.add, op1=ALU.add).then_inc(y_added, 1)

            def slot(m, i):
                if m == 2:
                    dve.wait_ge(x_lo, WO_FIRST)
                    for n, c, cols in weight_pieces(WO_FIRST):
                        split_lo(n, 0, wo[:, HI, c, cols], wo[:, LO, c, cols], W_COLS)
                for k in range(STEPS):
                    u, p = pair_at(m, k)
                    if there(u, i):
                        pair_max(u, p, i)
                    if k == 0:
                        if there(m - 3, i):
                            lse_part(m - 3, i, 0)
                        if there(m - 1, i):
                            queries_hi(m - 1, i)
                        if there(m - 3, i):
                            lse_part(m - 3, i, 1)
                        if there(m - 1, i):
                            queries_lo(m - 1, i)
                        if there(m - 3, i):
                            lse_part(m - 3, i, 2)
                    if k == 1 and there(m - 3, i):
                        lse_keep(m - 3, i)
                    if k in (1, 5) and there(m - 2, i):
                        small_max(m - 2, k // 4, i)
                    if k == max(Y_PRODUCTS) and there(m - Y_LAG, i):
                        add_output(m - Y_LAG, i)
                    if k == 5 and there(m - 2, i):
                        less_max(m - 2, i)
                    if k == 4 and there(m - 4, i):
                        heads_hi(m - 4, i)
                    if k in (4, 7) and there(m - 2, i):
                        small_sums(m - 2, k // 6, i)
                    if k == 4 and there(m - 4, i):
                        heads_lo(m - 4, i)
                    if m % QC == 0 and k < QC and there(m, i):
                        if k == 0:
                            if due(n_due := count(1, m, i)):
                                dve.wait_ge(q_acc, n_due)
                        split_hi(piece(m, i, k), i, xs[:, HI, k, :])

            dve.wait_ge(rows_set, RING)
            in_slots(dve, slot, 2)


WEIGHTS = {"k_txt": "to_k_w", "v_txt": "to_v_w", "k_obj": "to_k_object_w", "v_obj": "to_v_object_w",
           "k_oth": "to_k_others_w", "v_oth": "to_v_others_w", "k_ip": "to_k_ip_w", "v_ip": "to_v_ip_w",
           "wq": "to_q_w", "wo": "to_out_w"}


def build(nc, d):
    project_context(nc, d)
    attend(nc, d)


def kernel(**inputs):
    import numpy as _np
    import concourse.bacc as _bacc
    from concourse import mybir as _mybir
    from concourse.bass_utils import run_bass_kernel_spmd as _run

    x, context = _np.asarray(inputs["x"]), _np.asarray(inputs["ctx_2048"])
    host = {"xT": x.transpose(0, 2, 1), "ctxT": context.transpose(0, 2, 1)}
    by_channel = context.transpose(2, 0, 1)
    at = 0
    for g, n in (("txt", N_TXT), ("obj", N_OBJ), ("oth", N_OTH), ("rest", REST)):
        host[f"ctxT_{g}"] = by_channel[:, :, at:at + n].reshape(CTX, BATCH * n)
        at += n
    for name, source in WEIGHTS.items():
        host[name] = _np.asarray(inputs[f"L0_xattn_{source}"])
    host["wq"] = host["wq"].reshape(CH, QC, HPU, HD).transpose(0, 1, 3, 2).reshape(CH, CH)
    host["bias"] = _np.asarray(inputs["L0_xattn_to_out_b"]).reshape(QC, P).T
    bounds = [0, N_TXT, N_TXT + N_OBJ, SMALL, TOK]
    rows = _np.zeros((2 * GROUPS, TOK), _np.float32)
    for g in range(GROUPS):
        rows[[g, GROUPS + g], bounds[g]:bounds[g + 1]] = 1
    host["group_rows"] = rows
    host["ident"] = _np.eye(P, dtype=_np.float32)

    nc = _bacc.Bacc("TRN2", target_bir_lowering=False, num_devices=1)
    arrays, d = {}, {}
    for name, a in host.items():
        arrays[f"in_{name}"] = _np.ascontiguousarray(a)
        d[name] = nc.dram_tensor(f"in_{name}", a.shape, F32, kind="ExternalInput").ap()
    d["kT"] = nc.dram_tensor("kT", (BATCH, 2, CH, TOK), F32, kind="Internal").ap()
    for g, n in (("txt", N_TXT), ("obj", N_OBJ), ("oth", N_OTH), ("rest", REST)):
        d[f"v_{g}_rows"] = nc.dram_tensor(f"v_{g}_rows", (BATCH * n, CH), F32, kind="Internal").ap()
    d["v_ip_rows"] = nc.dram_tensor("v_ip_rows", (BATCH, TOK - P, CH), F32, kind="Internal").ap()
    d["yT"] = nc.dram_tensor("out_yT", (BATCH, CH, TOK), F32, kind="ExternalOutput").ap()
    build(nc, d)
    r = _run(nc, [arrays], core_ids=[0])
    return _np.ascontiguousarray(r.results[0]["out_yT"].transpose(0, 2, 1))
```
